# Optimizing a Trainium2 kernel written in Bass

```python
import numpy as np
import jax
import jax.numpy as jnp

def _softmax(x, axis=-1):
    return jax.nn.softmax(x, axis=axis)

def _gelu(x):
    return jax.nn.gelu(x, approximate=True)

def _silu(x):
    return jax.nn.silu(x)

def _sigmoid(x):
    return jax.nn.sigmoid(x)

def _layernorm(x, axis=-1, eps=1e-05):
    m = jnp.mean(x, axis=axis, keepdims=True)
    v = jnp.var(x, axis=axis, keepdims=True)
    return (x - m) / jnp.sqrt(v + eps)

def _scatter_add(tgt, idx, src, axis=0):
    return tgt.at[idx].add(src)

def _segment_sum(src, seg, n):
    return jax.ops.segment_sum(src, seg, n)
kernel_name = 'mk_gnn_ffn_d2_gnn_r8_697877'

def setup_inputs(seed: int=0):
    np.random.seed(seed)
    _w = jnp.asarray

    def _rec_inputs():
        import jax
        import jax.numpy as jnp
        _gk = jax.random.key(seed)
        x = -0.0001538 + 1 * jax.random.normal(jax.random.fold_in(_gk, 1), (1024, 768), jnp.float32)
        _s = jax.random.randint(jax.random.fold_in(_gk, 2), (8192,), 0, 1024, jnp.int32)
        _d = jax.random.randint(jax.random.fold_in(_gk, 3), (8192,), 0, 1024, jnp.int32)
        _loop = jnp.arange(1024, dtype=jnp.int32)
        src = jnp.concatenate([_s, _d, _loop])
        dst = jnp.concatenate([_d, _s, _loop])
        _o = jnp.argsort(dst, stable=True)
        src = src[_o]
        dst = dst[_o]
        edge_type_3 = jax.random.randint(jax.random.fold_in(_gk, 12), (17408,), 0, 3, jnp.int32)
        node_type_3 = jax.random.randint(jax.random.fold_in(_gk, 13), (1024,), 0, 3, jnp.int32)
        return (x, src, dst, edge_type_3, node_type_3)
    x, src, dst, edge_type_3, node_type_3 = _rec_inputs()

    def _L0_gnn_setup():
        import jax, jax.numpy as jnp
        import numpy as np
        NEG_SLOPE = 0.2
        EPS = 1e-16
        N_NODES = 1024
        N_EDGES = 8192
        D_IN = 768
        D_HID = 768
        H1 = 8
        H2 = 1

        def gat_layer(x, W, a_s, a_d, b, edge_index, concat):
            n = x.shape[0]
            H, C = a_s.shape
            h = (x @ W).reshape(n, H, C)
            src, dst = (edge_index[0], edge_index[1])
            alpha_s = jnp.einsum('nhc,hc->nh', h, a_s)
            alpha_d = jnp.einsum('nhc,hc->nh', h, a_d)
            e = jax.nn.leaky_relu(alpha_s[src] + alpha_d[dst], NEG_SLOPE)
            m = jax.ops.segment_max(e, dst, num_segments=n)
            e = jnp.exp(e - m[dst])
            denom = jax.ops.segment_sum(e, dst, num_segments=n)
            alpha = e / (denom[dst] + EPS)
            msg = h[src] * alpha[:, :, None]
            out = jax.ops.segment_sum(msg, dst, num_segments=n)
            out = out.reshape(n, H * C) if concat else out.mean(axis=1)
            return out + b
        key = jax.random.key(seed)
        ks = jax.random.split(key, 10)
        x = jax.random.normal(ks[0], (N_NODES, D_IN), dtype=jnp.float32)
        edge_list = jax.random.randint(ks[1], (2, N_EDGES), 0, N_NODES, dtype=jnp.int32)
        s = 0.05
        W1 = jax.random.normal(ks[2], (D_IN, H1 * D_HID), dtype=jnp.float32) * s
        a_src1 = jax.random.normal(ks[3], (H1, D_HID), dtype=jnp.float32) * s
        a_dst1 = jax.random.normal(ks[4], (H1, D_HID), dtype=jnp.float32) * s
        b1 = jnp.zeros((H1 * D_HID,), dtype=jnp.float32)
        W2 = jax.random.normal(ks[5], (H1 * D_HID, H2 * D_HID), dtype=jnp.float32) * s
        a_src2 = jax.random.normal(ks[6], (H2, D_HID), dtype=jnp.float32) * s
        a_dst2 = jax.random.normal(ks[7], (H2, D_HID), dtype=jnp.float32) * s
        b2 = jnp.zeros((H2 * D_HID,), dtype=jnp.float32)
        return {'x': x, 'W1': W1, 'a_src1': a_src1, 'a_dst1': a_dst1, 'b1': b1, 'W2': W2, 'a_src2': a_src2, 'a_dst2': a_dst2, 'b2': b2, 'edge_list': edge_list}
    _L0_gnn_all = _L0_gnn_setup()
    _L0_gnn_in = {k: v for k, v in _L0_gnn_all.items() if k in ('W1', 'a_src1', 'a_dst1', 'b1', 'W2', 'a_src2', 'a_dst2', 'b2')}
    del _L0_gnn_all

    def _L0_ffn_setup():
        import math
        import jax, jax.numpy as jnp
        import numpy as np
        NUM_EXPERTS = 8
        TOP_K = 2
        CAPACITY_FACTOR = 1.25
        H = 768
        INNER = 384
        B, S = (2, 256)
        key = jax.random.key(seed)
        ks = jax.random.split(key, 9)
        scale = 0.02
        x = jax.random.normal(ks[0], (B, S, H), dtype=jnp.float32)
        Wr = jax.random.normal(ks[1], (H, NUM_EXPERTS), dtype=jnp.float32) * scale
        w1 = jax.random.normal(ks[2], (NUM_EXPERTS, H, INNER), dtype=jnp.float32) * scale
        w3 = jax.random.normal(ks[3], (NUM_EXPERTS, H, INNER), dtype=jnp.float32) * scale
        w2 = jax.random.normal(ks[4], (NUM_EXPERTS, INNER, H), dtype=jnp.float32) * scale
        s1 = jax.random.normal(ks[5], (H, INNER), dtype=jnp.float32) * scale
        s3 = jax.random.normal(ks[6], (H, INNER), dtype=jnp.float32) * scale
        s2 = jax.random.normal(ks[7], (INNER, H), dtype=jnp.float32) * scale
        return {'x': x, 'Wr': Wr, 'w1': w1, 'w3': w3, 'w2': w2, 's1': s1, 's3': s3, 's2': s2}
    _L0_ffn_all = _L0_ffn_setup()
    _L0_ffn_in = {k: v for k, v in _L0_ffn_all.items() if k in ('Wr', 'w1', 'w3', 'w2', 's1', 's3', 's2')}
    del _L0_ffn_all

    def _L1_gnn_setup():
        import jax, jax.numpy as jnp
        import numpy as np
        NUM_NODES = 1250
        NUM_EDGES = 20000
        IN_CH = 768
        TYPE_DIM = 128
        HID = 768
        OUT = 768
        NUM_REL = 3
        NUM_NODE_TYPE = 3

        def _glorot(key, shape):
            fan_in, fan_out = (shape[-2], shape[-1])
            lim = (6.0 / (fan_in + fan_out)) ** 0.5
            return jax.random.uniform(key, shape, jnp.float32, -lim, lim)

        def rgcn_conv(h, src, dst, edge_type, w_rel, w_root, bias):
            num_nodes = h.shape[0]
            xw = jnp.einsum('nd,rde->rne', h, w_rel)
            msg = xw[edge_type, src]
            onehot = jax.nn.one_hot(edge_type, NUM_REL, dtype=h.dtype)
            count = jax.ops.segment_sum(onehot, dst, num_segments=num_nodes)
            inv = jnp.where(count > 0, 1.0 / jnp.maximum(count, 1.0), 0.0)
            msg = msg * inv[dst, edge_type][:, None]
            agg = jax.ops.segment_sum(msg, dst, num_segments=num_nodes)
            return agg + h @ w_root + bias
        key = jax.random.key(seed)
        ks = jax.random.split(key, 16)
        d1 = IN_CH + TYPE_DIM
        inp = {'x': jax.random.normal(ks[0], (NUM_NODES, IN_CH), jnp.float32), 'node_type': jax.random.randint(ks[1], (NUM_NODES,), 0, NUM_NODE_TYPE, jnp.int32), 'edge_index': jax.random.randint(ks[2], (2, NUM_EDGES), 0, NUM_NODES, jnp.int32), 'edge_type': jax.random.randint(ks[3], (NUM_EDGES,), 0, NUM_REL, jnp.int32), 'node_emb': jax.random.normal(ks[4], (NUM_NODE_TYPE, TYPE_DIM), jnp.float32), 'w_rel1': _glorot(ks[5], (NUM_REL, d1, d1)), 'w_root1': _glorot(ks[6], (d1, d1)), 'b1': jnp.zeros((d1,), jnp.float32), 'w_rel2': _glorot(ks[7], (NUM_REL, d1, HID)), 'w_root2': _glorot(ks[8], (d1, HID)), 'b2': jnp.zeros((HID,), jnp.float32), 'w_rel3': _glorot(ks[9], (NUM_REL, HID, OUT)), 'w_root3': _glorot(ks[10], (HID, OUT)), 'b3': jnp.zeros((OUT,), jnp.float32)}
        return inp
    _L1_gnn_all = _L1_gnn_setup()
    _L1_gnn_in = {k: v for k, v in _L1_gnn_all.items() if k in ('node_emb', 'w_rel1', 'w_root1', 'b1', 'w_rel2', 'w_root2', 'b2', 'w_rel3', 'w_root3', 'b3')}
    del _L1_gnn_all

    def _L1_ffn_setup():
        import jax, jax.numpy as jnp
        import numpy as np
        import math
        SQRT_2_OVER_PI = math.sqrt(2.0 / math.pi)

        def gelu(x):
            return x * 0.5 * (1.0 + jnp.tanh(SQRT_2_OVER_PI * (x + 0.044715 * x * x * x)))
        key = jax.random.key(seed)
        ks = jax.random.split(key, 6)
        B, S, D, M, E = (8, 512, 768, 384, 8)
        return {'x': jax.random.normal(ks[0], (B, S, D), dtype=jnp.float32), 'router_w': jax.random.normal(ks[1], (D, E), dtype=jnp.float32) * (1.0 / np.sqrt(D)), 'w1': jax.random.normal(ks[2], (E, D, M), dtype=jnp.float32) * (1.0 / np.sqrt(D)), 'b1': jax.random.normal(ks[3], (E, M), dtype=jnp.float32) * 1e-06, 'w2': jax.random.normal(ks[4], (E, M, D), dtype=jnp.float32) * (1.0 / np.sqrt(M)), 'b2': jax.random.normal(ks[5], (E, D), dtype=jnp.float32) * 1e-06}
    _L1_ffn_all = _L1_ffn_setup()
    _L1_ffn_in = {k: v for k, v in _L1_ffn_all.items() if k in ('router_w', 'w1', 'b1', 'w2', 'b2')}
    del _L1_ffn_all
    return {'x': x, 'src': src, 'dst': dst, 'edge_type_3': edge_type_3, 'node_type_3': node_type_3, 'L0_gnn_W1': _L0_gnn_in['W1'], 'L0_gnn_a_src1': _L0_gnn_in['a_src1'], 'L0_gnn_a_dst1': _L0_gnn_in['a_dst1'], 'L0_gnn_b1': _L0_gnn_in['b1'], 'L0_gnn_W2': _L0_gnn_in['W2'], 'L0_gnn_a_src2': _L0_gnn_in['a_src2'], 'L0_gnn_a_dst2': _L0_gnn_in['a_dst2'], 'L0_gnn_b2': _L0_gnn_in['b2'], 'L0_ffn_Wr': _L0_ffn_in['Wr'], 'L0_ffn_w1': _L0_ffn_in['w1'], 'L0_ffn_w3': _L0_ffn_in['w3'], 'L0_ffn_w2': _L0_ffn_in['w2'], 'L0_ffn_s1': _L0_ffn_in['s1'], 'L0_ffn_s3': _L0_ffn_in['s3'], 'L0_ffn_s2': _L0_ffn_in['s2'], 'L1_gnn_node_emb': _L1_gnn_in['node_emb'], 'L1_gnn_w_rel1': _L1_gnn_in['w_rel1'], 'L1_gnn_w_root1': _L1_gnn_in['w_root1'], 'L1_gnn_b1': _L1_gnn_in['b1'], 'L1_gnn_w_rel2': _L1_gnn_in['w_rel2'], 'L1_gnn_w_root2': _L1_gnn_in['w_root2'], 'L1_gnn_b2': _L1_gnn_in['b2'], 'L1_gnn_w_rel3': _L1_gnn_in['w_rel3'], 'L1_gnn_w_root3': _L1_gnn_in['w_root3'], 'L1_gnn_b3': _L1_gnn_in['b3'], 'L1_ffn_router_w': _L1_ffn_in['router_w'], 'L1_ffn_w1': _L1_ffn_in['w1'], 'L1_ffn_b1': _L1_ffn_in['b1'], 'L1_ffn_w2': _L1_ffn_in['w2'], 'L1_ffn_b2': _L1_ffn_in['b2']}

def reference(x, src, dst, edge_type_3, node_type_3, L0_gnn_W1, L0_gnn_a_src1, L0_gnn_a_dst1, L0_gnn_b1, L0_gnn_W2, L0_gnn_a_src2, L0_gnn_a_dst2, L0_gnn_b2, L0_ffn_Wr, L0_ffn_w1, L0_ffn_w3, L0_ffn_w2, L0_ffn_s1, L0_ffn_s3, L0_ffn_s2, L1_gnn_node_emb, L1_gnn_w_rel1, L1_gnn_w_root1, L1_gnn_b1, L1_gnn_w_rel2, L1_gnn_w_root2, L1_gnn_b2, L1_gnn_w_rel3, L1_gnn_w_root3, L1_gnn_b3, L1_ffn_router_w, L1_ffn_w1, L1_ffn_b1, L1_ffn_w2, L1_ffn_b2):
    import jax
    import jax.numpy as jnp

    def _L0_gnn_ref(x, W1, a_src1, a_dst1, b1, W2, a_src2, a_dst2, b2, edge_list):
        import jax, jax.numpy as jnp
        import numpy as np
        NEG_SLOPE = 0.2
        EPS = 1e-16
        N_NODES = 1024
        N_EDGES = 8192
        D_IN = 768
        D_HID = 768
        H1 = 8
        H2 = 1

        def gat_layer(x, W, a_s, a_d, b, edge_index, concat):
            n = x.shape[0]
            H, C = a_s.shape
            h = (x @ W).reshape(n, H, C)
            src, dst = (edge_index[0], edge_index[1])
            alpha_s = jnp.einsum('nhc,hc->nh', h, a_s)
            alpha_d = jnp.einsum('nhc,hc->nh', h, a_d)
            e = jax.nn.leaky_relu(alpha_s[src] + alpha_d[dst], NEG_SLOPE)
            m = jax.ops.segment_max(e, dst, num_segments=n)
            e = jnp.exp(e - m[dst])
            denom = jax.ops.segment_sum(e, dst, num_segments=n)
            alpha = e / (denom[dst] + EPS)
            msg = h[src] * alpha[:, :, None]
            out = jax.ops.segment_sum(msg, dst, num_segments=n)
            out = out.reshape(n, H * C) if concat else out.mean(axis=1)
            return out + b
        h = gat_layer(x, W1, a_src1, a_dst1, b1, edge_list, concat=True)
        h = jax.nn.elu(h)
        out = gat_layer(h, W2, a_src2, a_dst2, b2, edge_list, concat=True)
        return out

    def _L0_ffn_ref(x, Wr, w1, w3, w2, s1, s3, s2):
        import math
        import jax, jax.numpy as jnp
        import numpy as np
        NUM_EXPERTS = 8
        TOP_K = 2
        CAPACITY_FACTOR = 1.25
        H = 768
        INNER = 384
        B, S = (2, 256)
        b, s, h = x.shape
        n = b * s
        flat = x.reshape(n, h)
        logits = flat @ Wr
        probs = jax.nn.softmax(logits, axis=-1)
        topk_p, topk_i = jax.lax.top_k(probs, TOP_K)
        topk_p = topk_p / jnp.clip(topk_p.sum(-1, keepdims=True), 1e-09)
        capacity = max(1, math.ceil(n * TOP_K / NUM_EXPERTS * CAPACITY_FACTOR))
        onehot = topk_i[None, :, :] == jnp.arange(NUM_EXPERTS)[:, None, None]
        w_tok = jnp.sum(topk_p[None] * onehot, axis=-1)
        assigned = jnp.any(onehot, axis=-1)
        score = jnp.where(assigned, w_tok, -jnp.inf)
        order = jnp.argsort(-score, axis=1)[:, :capacity]
        score_sel = jnp.take_along_axis(score, order, axis=1)
        valid = jnp.isfinite(score_sel)
        weight_sel = jnp.where(valid, score_sel, 0.0)
        dispatch = flat[order]
        gate = jax.nn.silu(jnp.einsum('ech,ehi->eci', dispatch, w1))
        up = jnp.einsum('ech,ehi->eci', dispatch, w3)
        expert_out = jnp.einsum('eci,eih->ech', gate * up, w2)
        expert_out = expert_out * weight_sel[..., None]
        routed = jnp.zeros((n, h), dtype=flat.dtype)
        routed = routed.at[order.reshape(-1)].add(expert_out.reshape(-1, h))
        shared = jax.nn.silu(flat @ s1) * (flat @ s3) @ s2
        out = routed + shared
        return out.reshape(b, s, h)

    def _L1_gnn_ref(x, node_type, edge_index, edge_type, node_emb, w_rel1, w_root1, b1, w_rel2, w_root2, b2, w_rel3, w_root3, b3):
        import jax, jax.numpy as jnp
        import numpy as np
        NUM_NODES = 1250
        NUM_EDGES = 20000
        IN_CH = 768
        TYPE_DIM = 128
        HID = 768
        OUT = 768
        NUM_REL = 3
        NUM_NODE_TYPE = 3

        def _glorot(key, shape):
            fan_in, fan_out = (shape[-2], shape[-1])
            lim = (6.0 / (fan_in + fan_out)) ** 0.5
            return jax.random.uniform(key, shape, jnp.float32, -lim, lim)

        def rgcn_conv(h, src, dst, edge_type, w_rel, w_root, bias):
            num_nodes = h.shape[0]
            xw = jnp.einsum('nd,rde->rne', h, w_rel)
            msg = xw[edge_type, src]
            onehot = jax.nn.one_hot(edge_type, NUM_REL, dtype=h.dtype)
            count = jax.ops.segment_sum(onehot, dst, num_segments=num_nodes)
            inv = jnp.where(count > 0, 1.0 / jnp.maximum(count, 1.0), 0.0)
            msg = msg * inv[dst, edge_type][:, None]
            agg = jax.ops.segment_sum(msg, dst, num_segments=num_nodes)
            return agg + h @ w_root + bias
        src, dst = (edge_index[0], edge_index[1])
        h = jnp.concatenate([x, node_emb[node_type]], axis=-1)
        h = jax.nn.relu(rgcn_conv(h, src, dst, edge_type, w_rel1, w_root1, b1))
        h = jax.nn.relu(rgcn_conv(h, src, dst, edge_type, w_rel2, w_root2, b2))
        h = jax.nn.relu(rgcn_conv(h, src, dst, edge_type, w_rel3, w_root3, b3))
        return h

    def _L1_ffn_ref(x, router_w, w1, b1, w2, b2):
        import jax, jax.numpy as jnp
        import numpy as np
        import math
        SQRT_2_OVER_PI = math.sqrt(2.0 / math.pi)

        def gelu(x):
            return x * 0.5 * (1.0 + jnp.tanh(SQRT_2_OVER_PI * (x + 0.044715 * x * x * x)))
        B, S, D = x.shape
        E = router_w.shape[1]
        T = B * S
        C = T // E
        xf = x.reshape(T, D)
        router_logits = xf @ router_w
        router_probs = jax.nn.softmax(router_logits, axis=-1)
        expert_gate = jnp.max(router_probs, axis=-1)
        expert_index = jnp.argmax(router_probs, axis=-1)
        expert_mask = jax.nn.one_hot(expert_index, E, dtype=xf.dtype)
        position_in_expert = (jnp.cumsum(expert_mask, axis=0) * expert_mask).astype(jnp.int32)
        expert_mask = expert_mask * (position_in_expert < C).astype(xf.dtype)
        expert_mask_flat = jnp.sum(expert_mask, axis=-1)
        expert_gate = expert_gate * expert_mask_flat
        combine = (expert_gate * expert_mask_flat)[:, None, None] * jax.nn.one_hot(expert_index, E, dtype=xf.dtype)[:, :, None] * jax.nn.one_hot(position_in_expert, C, dtype=xf.dtype)
        dispatch = (combine != 0).astype(xf.dtype)
        expert_inputs = jnp.einsum('td,tec->ecd', xf, dispatch)
        h = gelu(jnp.einsum('ecd,edm->ecm', expert_inputs, w1) + b1[:, None, :])
        expert_outputs = gelu(jnp.einsum('ecm,emd->ecd', h, w2) + b2[:, None, :])
        out = jnp.einsum('ecd,tec->td', expert_outputs, combine)
        return out.reshape(B, S, D)
    edge_index = jnp.stack([src, dst])
    x = x + _L0_gnn_ref(_layernorm(x, axis=-1), L0_gnn_W1, L0_gnn_a_src1, L0_gnn_a_dst1, L0_gnn_b1, L0_gnn_W2, L0_gnn_a_src2, L0_gnn_a_dst2, L0_gnn_b2, edge_index)
    x = x + _L0_ffn_ref(_layernorm(x, axis=-1)[None], L0_ffn_Wr, L0_ffn_w1, L0_ffn_w3, L0_ffn_w2, L0_ffn_s1, L0_ffn_s3, L0_ffn_s2)[0]
    x = x + _L1_gnn_ref(_layernorm(x, axis=-1), node_type_3, edge_index, edge_type_3, L1_gnn_node_emb, L1_gnn_w_rel1, L1_gnn_w_root1, L1_gnn_b1, L1_gnn_w_rel2, L1_gnn_w_root2, L1_gnn_b2, L1_gnn_w_rel3, L1_gnn_w_root3, L1_gnn_b3)
    x = x + _L1_ffn_ref(_layernorm(x, axis=-1)[None], L1_ffn_router_w, L1_ffn_w1, L1_ffn_b1, L1_ffn_w2, L1_ffn_b2)[0]
    return x

_drawn_inputs = setup_inputs


def setup_inputs(seed=0):
    import zlib

    import numpy as np

    out = dict(_drawn_inputs(seed))
    spreads = {'L0_gnn_b1': (0.0, 0.1),
     'L0_gnn_b2': (0.0, 0.1),
     'L1_gnn_b1': (0.0, 0.1),
     'L1_gnn_b2': (0.0, 0.1),
     'L1_gnn_b3': (0.0, 0.271)}
    factors = {'L0_ffn_Wr': 3.095,
     'L0_ffn_w1': 2.848,
     'L0_ffn_w3': 2.795,
     'L0_ffn_w2': 2.787,
     'L1_ffn_b1': 8.0,
     'L1_ffn_b2': 8.0}
    for name, (base, spread) in spreads.items():
        noise = np.random.default_rng([zlib.crc32(name.encode()), seed]).standard_normal(out[name].shape)
        drawn = base * np.exp(spread * noise) if base else spread * noise
        out[name] = jnp.asarray(drawn.astype(out[name].dtype))
    for name, factor in factors.items():
        out[name] = (out[name] * factor).astype(out[name].dtype)
    return out
```

```python
import concourse.bass as bass
from concourse import mybir
from contextlib import ExitStack

fp32 = mybir.dt.float32
bf16 = mybir.dt.bfloat16
fp16 = mybir.dt.float16
i32 = mybir.dt.int32
u32 = mybir.dt.uint32
u16 = mybir.dt.uint16
ALU = mybir.AluOpType
ACT = mybir.ActivationFunctionType
AX = mybir.AxisListType
MULT, ADD, SUB, MAX, MIN = ALU.mult, ALU.add, ALU.subtract, ALU.max, ALU.min


class Chain:

    def __init__(self, eng, sem):
        self.eng, self.sem, self.base, self.k = eng, sem, 0, 0

    def step(self, ins):
        self.k += 1
        return ins.then_inc(self.sem, 1)

    def sync(self):
        self.eng.wait_ge(self.sem, self.base + self.k)

    def turn(self, i, first, per):
        if self.k or isinstance(self.base, int):
            self.before = self.base + self.k
        self.base, self.k = (i - first) * per + self.before, 0

    def leave(self, turns, per):
        assert self.k == per, (self.k, per)
        self.base, self.k = self.before + turns * per, 0


def build(nc, io, out, dbg=None):
    P = 128
    N, D = io['x'].shape
    E, = io['src'].shape
    NT = N // P
    KD = D // P
    R = 3
    NBK = R * NT
    EC = E // P
    NCH = EC + NBK
    H1 = io['L0_gnn_a_src1'].shape[0]
    HD = D // 2
    NH = N // 2
    NEG = -1e30
    EPS = 1e-5
    NX = io['L0_ffn_Wr'].shape[1]
    M0 = io['L0_ffn_s1'].shape[1]
    KM = M0 // P
    CAP0 = -(-N * 2 * 5 // (NX * 4))
    CB0 = [(b, min(P, CAP0 - b)) for b in range(0, CAP0, P)]
    C1 = N // NX
    TD = io['L1_gnn_node_emb'].shape[1]
    RG = [('L1_gnn_w_rel1', 'L1_gnn_w_root1', 'L1_gnn_b1'),
          ('L1_gnn_w_rel2', 'L1_gnn_w_root2', 'L1_gnn_b2'),
          ('L1_gnn_w_rel3', 'L1_gnn_w_root3', 'L1_gnn_b3')]
    RIN = [io[w].shape[0] for _, w, _ in RG]
    ROUT = [io[w].shape[1] for _, w, _ in RG]
    assert EC * P == E and CAP0 == 320 and NBK * P + E <= NCH * P

    ctx = ExitStack()
    with ctx:
        def sb(name, shape, dt=fp32):
            return ctx.enter_context(nc.sbuf_tensor(name, shape, dt))

        def sem(name):
            return ctx.enter_context(nc.semaphore(name))

        def scratch(name, shape, dt=fp32):
            return nc.dram_tensor(name, shape, dt, kind="Internal").ap()

        slots = scratch("slots", [P * NCH, 1], i32)
        adj_d = scratch("adj_d", [R, P, NT * N], u16)
        disp0_d = scratch("disp0_d", [NX * CAP0, D])
        eout0_d = scratch("eout0_d", [NX * CAP0, D])
        disp1_d = scratch("disp1_d", [NX * C1, D])
        eout1_d = scratch("eout1_d", [NX * C1, D])
        x2_d = scratch("x2_d", [N, D])

        ones = sb("ones", [P, P])
        ident = sb("ident", [P, P])
        before = sb("before", [P, P])
        iota8 = sb("iota8", [P, 8])
        WORDS = 51712
        arena = sb("arena", [P, WORDS])

        def cut(at, shape, dt=fp32):
            n = 1
            for s in shape:
                n *= s
            per = {fp32: 1, i32: 1, u32: 1, bf16: 2, fp16: 2, u16: 2}[dt]
            v = arena[:, at:at + n // per]
            assert at + n // per <= WORDS
            if dt != fp32:
                v = v.bitcast(dt)
            if len(shape) == 2:
                v = v.rearrange("p (a b) -> p a b", a=shape[0])
            if len(shape) == 3:
                v = v.rearrange("p (a b c) -> p a b c", a=shape[0], b=shape[1])
            return v

        XT = cut(0, [KD, N])
        AT = cut(6144, [NT, N], u16)
        MK = cut(10240, [NT, N], bf16)
        H = cut(14336, [NT, D])
        PM = cut(20480, [NT, N])
        a_bc = cut(20480, [2, D])
        diag = cut(22016, [3, N])
        junk = cut(25088, [N])
        OT = cut(28672, [KD, N])
        ACC = cut(34816, [NT, D])
        W1 = cut(40960, [KD, D])
        W2 = cut(45568, [KD, D])
        ET = cut(50176, [2, NH])
        RD = cut(51200, [NH])
        XN = cut(0, [NT, D])
        b2_bc = cut(40960, [D])
        XL = cut(14336, [NT, D])
        A_r = cut(20480, [NBK * N], u16)
        onehot = cut(34816, [NBK, EC])
        running = cut(45568, [NBK, EC])
        o = 38080
        edges = cut(o, [3, EC], i32)
        ework = cut(o + 408, [5, EC], i32)
        keyf = cut(o + 1088, [EC])
        slotf = cut(o + 1224, [EC])
        sloti = cut(o + 1360, [3, EC], i32)
        row = cut(o + 1768, [EC], i32)
        empty = cut(o + 1904, [NCH], i32)
        recs = cut(o + 2064, [3, NCH], i32)
        cmp = cut(10240, [NCH, NBK])
        iota = cut(6144, [N])
        zero = cut(0, [D])
        D1 = cut(48832, [2, N], bf16)
        S1 = cut(48832 + 1024, [2, P], bf16)
        MN = cut(45568, [NT, N], bf16)
        iotah = cut(50176, [N], fp16)
        recf = cut(50688, [2, NCH])
        bk = cut(51008, [10, NBK + 1])
        bki = cut(51258, [NBK], i32)
        boff = cut(51282, [NCH])
        boffi = cut(51442, [NCH], i32)

        LN = cut(6144, [NT, D])
        LT = cut(12288, [KD, N])
        EW = [(cut(18432 + 6912 * b, [KD, M0]), cut(20736 + 6912 * b, [KD, M0]), cut(23040 + 6912 * b, [KM, D])) for b in range(2)]
        SA = cut(25344, [KM, N])
        SG = cut(28416, [2, NH])
        SW = (cut(32256, [KD, M0]), cut(34560, [KD, M0]), cut(36864, [KM, D]))
        DR = [cut(39168 + 2304 * b, [len(CB0), D]) for b in range(2)]
        DT = cut(43776, [KD, CAP0])
        EA = cut(45696, [KM, CAP0])
        EG = cut(46656, [2, CAP0])
        EO = cut(47296, [len(CB0), D])
        rowsT = cut(43776, [3, N])
        rjunk = cut(46848, [N])
        earlier = cut(49600, [2 * N - P], bf16)
        rt = cut(50560, [10, NT, NX])
        Wr = cut(51328, [KD, NX])
        rk = cut(51376, [12, 2, NT])
        m8 = cut(51568, [NT, 8])
        ix = cut(51632, [NT, 8], u32)
        GR = [cut(6144 + D * b, [D]) for b in range(4)]
        YT = cut(6144, [RIN[0] // P, N])
        RA = cut(13312, [NT, ROUT[0]])
        AF = cut(20480, [NT, N])
        AR = cut(28672, [NT * N], u16)
        RW = 32768
        inv = cut(39040, [R, N])
        bias_bc = cut(42112, [ROUT[0]])
        HN = 43008
        emb = cut(50176, [R, TD])
        GW = [(cut(18432 + 4608 * b, [KD, M0]), cut(20736 + 4608 * b, [KM, D])) for b in range(2)]
        GB = [cut(27648 + D * b, [D]) for b in range(2)]
        GD = [cut(29184 + D * b, [D]) for b in range(2)]
        GT = cut(30720, [KD, C1])
        GA = cut(31488, [KM, C1])
        GO = cut(31872, [2, D])
        gb1 = [cut(33408 + 4 * b, [KM]) for b in range(2)]

        idx = sb("idx", [P, 2, 2, NT], i32)
        rjunk2 = cut(50560, [2, NH])
        ntype = sb("ntype", [P, NT], i32)
        ntypef = sb("ntypef", [P, NT])
        identb = sb("identb", [P, P], bf16)
        alpha = sb("alpha", [P, 2, NT])
        alpha_low = sb("alpha_low", [P, NT])
        mx = sb("mx", [P, 4, NT])
        b1c = sb("b1c", [P, KD])
        stats = sb("stats", [P, NT, 2, 6])
        mv = sb("mv", [P, NT, 2])
        rstd = sb("rstd", [P, NT])
        rd2 = sb("rd2", [P, NT])

        psum = ctx.enter_context(nc.psum_tensor("psum", [P, 8, 512], fp32))

        s_edges = sem("s_edges")
        s_const = sem("s_const")
        dch = sem("dch")
        ach = sem("ach")
        s_cnt = sem("s_cnt")
        s_tot = sem("s_tot")
        s_empty = sem("s_empty")
        s_pre = sem("s_pre")
        s_row = sem("s_row")
        s_scat = sem("s_scat")
        s_recs = sem("s_recs")
        s_hot = sem("s_hot")
        s_pair = sem("s_pair")
        s_added = sem("s_added")
        s_azero = sem("s_azero")
        s_x = sem("s_x")
        s_zero = sem("s_zero")
        s_var = sem("s_var")
        s_std = sem("s_std")
        s_ln = sem("s_ln")
        s_xt_mm = sem("s_xt_mm")
        s_xt_ev = sem("s_xt_ev")
        s_spill = sem("s_spill")
        s_mn = sem("s_mn")
        s_mk_mm = sem("s_mk_mm")
        s_mk_ev = sem("s_mk_ev")
        s_w1 = sem("s_w1")
        s_w2 = sem("s_w2")
        s_a = sem("s_a")
        s_b1 = sem("s_b1")
        s_h_mm = sem("s_h_mm")
        s_h_ev = sem("s_h_ev")
        s_diag = sem("s_diag")
        s_bc = sem("s_bc")
        s_rows = sem("s_rows")
        s_larger = sem("s_larger")
        s_exp = sem("s_exp")
        s_P = sem("s_P")
        s_p_mm = sem("s_p_mm")
        s_acc_ev = sem("s_acc_ev")
        s_agg_mm = sem("s_agg_mm")
        s_agg_ev = sem("s_agg_ev")
        s_elu = sem("s_elu")
        s_efix = sem("s_efix")
        s_ot = sem("s_ot")
        s_xr = sem("s_xr")
        s_g2_mm = sem("s_g2_mm")
        s_x1 = sem("s_x1")
        s_at = sem("s_at")
        s_wr = sem("s_wr")
        s_sw = sem("s_sw")
        s_tri = sem("s_tri")
        s_lg = sem("s_lg")
        s_ct = sem("s_ct")
        s_exps = sem("s_exps")
        s_rt_in = sem("s_rt_in")
        s_rt_mm = sem("s_rt_mm")
        s_rt_ev = sem("s_rt_ev")
        s_rr_mm = sem("s_rr_mm")
        s_rank = sem("s_rank")
        s_idx = sem("s_idx")
        s_disp = sem("s_disp")
        s_sg_mm = sem("s_sg_mm")
        s_ssilu = sem("s_ssilu")
        s_sact = sem("s_sact")
        s_so_mm = sem("s_so_mm")
        s_so_ev = sem("s_so_ev")
        s_ew0 = sem("s_ew0")
        s_ew1 = sem("s_ew1")
        s_dr0 = sem("s_dr0")
        s_dr1 = sem("s_dr1")
        s_dt_mm = sem("s_dt_mm")
        s_dt_ev = sem("s_dt_ev")
        s_gu_mm = sem("s_gu_mm")
        s_silu = sem("s_silu")
        s_act = sem("s_act")
        s_eo_mm = sem("s_eo_mm")
        s_eo_ev = sem("s_eo_ev")
        s_es = sem("s_es")
        s_ga0 = sem("s_ga0")
        s_ga1 = sem("s_ga1")
        s_ga2 = sem("s_ga2")
        s_ga3 = sem("s_ga3")
        s_comb = sem("s_comb")
        s_emb = sem("s_emb")
        s_hn = sem("s_hn")
        s_y_mm = sem("s_y_mm")
        s_y_ev = sem("s_y_ev")
        s_z_mm = sem("s_z_mm")
        s_z_ev = sem("s_z_ev")
        s_rw = sem("s_rw")
        s_ar = sem("s_ar")
        s_af = sem("s_af")
        s_rb = sem("s_rb")
        s_relu = sem("s_relu")
        s_x3 = sem("s_x3")
        s_ft_mm = sem("s_ft_mm")
        s_ft_ev = sem("s_ft_ev")
        s_f1_mm = sem("s_f1_mm")
        s_f1 = sem("s_f1")
        s_f2_mm = sem("s_f2_mm")
        s_f2 = sem("s_f2")
        s_f3 = sem("s_f3")
        s_fs0 = sem("s_fs0")
        s_fs1 = sem("s_fs1")
        s_fw0 = sem("s_fw0")
        s_fw1 = sem("s_fw1")
        s_fr0 = sem("s_fr0")
        s_fr1 = sem("s_fr1")
        s_disp1 = sem("s_disp1")
        s_out = sem("s_out")

        block = ctx.enter_context(nc.Block())
        w1_v = io['L0_gnn_W1'].rearrange("(k p) (h c) -> h p k c", p=P, h=H1)
        w2_v = io['L0_gnn_W2'].rearrange("(h k p) c -> h p k c", p=P, h=H1)
        b1_v = io['L0_gnn_b1'].rearrange("(h m p) -> h p m", p=P, h=H1)

        def bank(b, n=512):
            return psum[:, b, 0:n]

        @block.sync
        def _(sp):
            for n, a in enumerate((io['src'], io['dst'], io['edge_type_3'])):
                sp.dma_start(edges[:, n, :], a.rearrange("(p c) -> p c", p=P)).then_inc(s_edges, 16)
            sp.dma_start(XL, io['x'].rearrange("(t p) d -> p t d", p=P)).then_inc(s_x, 16)
            sp.wait_ge(s_empty, 1)
            sp.dma_start(slots.rearrange("(p c) o -> p (c o)", p=P), empty).then_inc(s_pre, 16)
            sp.dma_start(W1, w1_v[0]).then_inc(s_w1, 16)
            sp.wait_ge(s_empty, 2)
            for buf in (disp0_d, disp1_d):
                rows = buf.rearrange("(n p) d -> n p d", p=P)
                for n in range(rows.shape[0]):
                    sp.dma_start(rows[n], zero).then_inc(s_zero, 16)
            sp.dma_start(b1c[:, :], b1_v[0], allow_slow_non_contiguous=True).then_inc(s_b1, 16)
            sp.wait_ge(s_scat, 16 * EC)
            sp.dma_start(recs[:, 0, :], slots.rearrange("(p c) o -> p (c o)", p=P)).then_inc(s_recs, 16)
            sp.wait_ge(s_added, NCH)
            for r in range(R):
                sp.dma_start(adj_d[r], A_r[:, r * NT * N:(r + 1) * NT * N]).then_inc(s_spill, 16)
            sp.wait_ge(s_spill, 16 * R)
            sp.wait_ge(s_at, 1)

            def load_a(i):
                for k, name in enumerate(('L0_gnn_a_src1', 'L0_gnn_a_dst1')):
                    sp.dma_start(a_bc[:, k, :], io[name][bass.ds(i, 1), :].rearrange("o d -> (o d)").partition_broadcast(P)).then_inc(s_a, 16)

            load_a(0)

            def head_loads(i, first=False, last=False):
                if not last:
                    sp.wait_ge(s_h_mm, (i + 1) * 16)
                    sp.dma_start(W1, w1_v[bass.ds(i + 1, 1)].rearrange("o p k c -> (o p) k c")).then_inc(s_w1, 16)
                if not first:
                    sp.wait_ge(s_p_mm, i * 16)
                sp.dma_start(W2, w2_v[bass.ds(i, 1)].rearrange("o p k c -> (o p) k c")).then_inc(s_w2, 16)
                if not last:
                    sp.wait_ge(s_agg_mm, (i + 1) * 14)
                    load_a(i + 1)
                    sp.wait_ge(s_elu, (i + 1) * 12)
                    sp.dma_start(b1c[:, :], b1_v[bass.ds(i + 1, 1)].rearrange("o p m -> (o p) m"), allow_slow_non_contiguous=True).then_inc(s_b1, 16)

            sp.wait_ge(s_mk_ev, 8)
            head_loads(0, first=True)
            with sp.Fori(1, H1 - 1) as i:
                head_loads(i)
            head_loads(H1 - 1, last=True)
            sp.wait_ge(s_agg_mm, H1 * 14)
            for k, name in enumerate(('L0_gnn_a_src2', 'L0_gnn_a_dst2')):
                sp.dma_start(a_bc[:, k, :], io[name].rearrange("o d -> (o d)").partition_broadcast(P)).then_inc(s_a, 16)
            sp.wait_ge(s_h_mm, H1 * 16)
            sp.dma_start(XN, io['x'].rearrange("(t p) d -> p t d", p=P)).then_inc(s_xr, 16)
            sp.wait_ge(s_ot, H1 * 12)
            sp.dma_start(b2_bc, io['L0_gnn_b2'].partition_broadcast(P)).then_inc(s_xr, 16)

            sp.wait_ge(s_x1, 16)
            sp.dma_start(Wr, io['L0_ffn_Wr'].rearrange("(k p) e -> p k e", p=P)).then_inc(s_wr, 16)
            for w, name in zip(SW, ('L0_ffn_s1', 'L0_ffn_s3', 'L0_ffn_s2')):
                sp.dma_start(w, io[name].rearrange("(k p) n -> p k n", p=P)).then_inc(s_sw, 16)
            ew_v = [io[name].rearrange("e (k p) n -> e p k n", p=P) for name in ('L0_ffn_w1', 'L0_ffn_w3', 'L0_ffn_w2')]
            s_ew, s_dr = (s_ew0, s_ew1), (s_dr0, s_dr1)

            def expert_loads(e, b, reuse):
                if reuse:
                    sp.wait_ge(s_eo_mm, (e - 1) * 6)
                for w, v in zip(EW[b], ew_v):
                    sp.dma_start(w, v[bass.ds(e, 1)].rearrange("o p k n -> (o p) k n")).then_inc(s_ew[b], 16)
                if not reuse:
                    sp.wait_ge(s_disp, 16 * 2 * NT)
                for j, (c0, cn) in enumerate(CB0):
                    sp.dma_start(DR[b][0:cn, j, :], disp0_d[bass.ds(e * CAP0 + c0, cn), :]).then_inc(s_dr[b], 16)

            expert_loads(0, 0, False)
            sp.wait_ge(s_so_mm, 16)
            expert_loads(1, 1, False)
            with sp.Fori(1, NX // 2) as i:
                expert_loads(i * 2, 0, True)
                expert_loads(i * 2 + 1, 1, True)

            sp.dma_start(ntype[:, :], io['node_type_3'].rearrange("(t p) -> p t", p=P), allow_slow_non_contiguous=True).then_inc(s_emb, 16)
            sp.wait_ge(s_eo_ev, 6 * NX)
            sp.wait_ge(s_es, 48 * NX)
            sp.dma_start(emb.rearrange("p a b -> p (a b)"), io['L1_gnn_node_emb'].rearrange("a b -> (a b)").partition_broadcast(P)).then_inc(s_emb, 16)
            for lay in range(3):
                ft, fo = RIN[lay] // P, ROUT[lay]
                rel, root, bias = (io[n] for n in RG[lay])
                w_ = cut(RW, [ft, fo])
                if lay:
                    sp.wait_ge(s_z_ev, lay * 64 - 48)
                sp.dma_start(bias_bc[:, 0:fo], bias.partition_broadcast(P)).then_inc(s_rb, 16)
                if lay:
                    sp.wait_ge(s_z_mm, lay * 64)
                sp.dma_start(w_, root.rearrange("(k p) n -> p k n", p=P)).then_inc(s_rw, 16)
                rel_v = rel.rearrange("r (k p) n -> r p k n", p=P)

                def relation_loads(r, first=False):
                    if not first:
                        sp.wait_ge(s_af, r + lay * R)
                    sp.dma_start(AR, adj_d[bass.ds(r, 1)].rearrange("o p n -> (o p) n")).then_inc(s_ar, 16)
                    sp.wait_ge(s_z_mm, (r + 1) * 16 + lay * 64)
                    sp.dma_start(w_, rel_v[bass.ds(r, 1)].rearrange("o p k n -> (o p) k n")).then_inc(s_rw, 16)
                relation_loads(0, first=lay == 0)
                with sp.Fori(1, R) as r:
                    relation_loads(r)

            sp.wait_ge(s_x3, 16)
            sp.dma_start(Wr, io['L1_ffn_router_w'].rearrange("(k p) e -> p k e", p=P)).then_inc(s_wr, 16)
            fw_v = [io[name].rearrange("e (k p) n -> e p k n", p=P) for name in ('L1_ffn_w1', 'L1_ffn_w2')]
            fb_v = io['L1_ffn_b1'].rearrange("e (m p) -> e p m", p=P)
            s_fw, s_fr = (s_fw0, s_fw1), (s_fr0, s_fr1)

            def expert1_loads(e, b, reuse):
                if reuse:
                    sp.wait_ge(s_f2, (e - 1) * 2)
                for w, v in zip(GW[b], fw_v):
                    sp.dma_start(w, v[bass.ds(e, 1)].rearrange("o p k n -> (o p) k n")).then_inc(s_fw[b], 16)
                sp.dma_start(gb1[b], fb_v[bass.ds(e, 1)].rearrange("o p m -> (o p) m"), allow_slow_non_contiguous=True).then_inc(s_fw[b], 16)
                sp.dma_start(GB[b], io['L1_ffn_b2'][bass.ds(e, 1), :].rearrange("o d -> (o d)").partition_broadcast(P)).then_inc(s_fw[b], 16)
                if not reuse:
                    sp.wait_ge(s_disp1, 16 * NT)
                sp.dma_start(GD[b], disp1_d[bass.ds(e * C1, C1), :]).then_inc(s_fr[b], 16)

            expert1_loads(0, 0, False)
            expert1_loads(1, 1, False)
            with sp.Fori(1, NX // 2) as i:
                expert1_loads(i * 2, 0, True)
                expert1_loads(i * 2 + 1, 1, True)
            sp.wait_ge(s_comb, 2 * NT + NT)
            sp.dma_start(out.rearrange("(t p) d -> p t d", p=P), XN).then_inc(s_out, 16)
            sp.wait_ge(s_out, 16)

        @block.gpsimd
        def _(pool):
            pool.memset(empty, -1).then_inc(s_empty, 1)
            pool.memset(zero, 0.0).then_inc(s_empty, 1)
            pool.memset(ones[:, :], 1.0).then_inc(s_const, 1)
            pool.iota(iota, [[1, N]], base=0, channel_multiplier=0, allow_small_or_imprecise_dtypes=True).then_inc(s_const, 1)
            pool.iota(iota8[:, :], [[1, 8]], base=0, channel_multiplier=0, allow_small_or_imprecise_dtypes=True).then_inc(s_const, 1)
            pool.wait_ge(s_const, 3)
            pool.affine_select(out=before[:, :], in_=ones[:, :], compare_op=ALU.is_gt, fill=0.0,
                               base=0, pattern=[[1, P]], channel_multiplier=-1).then_inc(s_const, 1)
            pool.affine_select(out=ident[:, :], in_=ones[:, :], compare_op=ALU.is_equal, fill=0.0,
                               base=0, pattern=[[1, P]], channel_multiplier=-1).then_inc(s_const, 1)
            pool.memset(A_r, 0).then_inc(s_azero, 1)
            pool.wait_ge(s_row, 1)
            pool.wait_ge(s_pre, 16)
            for c in range(EC):
                pool.indirect_dma_start(slots, bass.IndirectOffsetOnAxis(ap=row[:, c:c + 1], axis=0),
                                        ework[:, 2, c:c + 1], None).then_inc(s_scat, 16)

            def elu_sums(i):
                for g in range(2 * KD):
                    hf, f = g // KD, g % KD
                    o_ = OT[:, f, hf * NH:(hf + 1) * NH]
                    pool.wait_ge(s_efix, i * 12 + g + 1)
                    pool.tensor_tensor(o_, o_, ET[:, g % 2, :], ADD).then_inc(s_ot, 1)

            elu_sums(0)
            with pool.Fori(1, H1) as i:
                elu_sums(i)

            pool.wait_ge(s_P, H1 * 2 + 2)
            pool.affine_select(out=earlier, in_=ones[:, 0:1].to_broadcast([P, 2 * N - P]), compare_op=ALU.is_gt, fill=0.0,
                               base=N - P, pattern=[[-1, 2 * N - P]], channel_multiplier=1).then_inc(s_tri, 1)
            s_ga = (s_ga0, s_ga1, s_ga2, s_ga3)

            def scatter(k, t, rows, s):
                pool.indirect_dma_start(rows, bass.IndirectOffsetOnAxis(ap=idx[:, 0, k, t:t + 1], axis=0), LN[:, t, :], None,
                                        bounds_check=rows.shape[0] - 1, oob_is_err=False).then_inc(s, 16)

            def gather(n, k, t, rows, base):
                if n >= 4:
                    pool.wait_ge(s_comb, base + n - 3)
                pool.indirect_dma_start(GR[n % 4], None, rows, bass.IndirectOffsetOnAxis(ap=idx[:, 1, k, t:t + 1], axis=0)).then_inc(s_ga[n % 4], 16)

            pool.wait_ge(s_zero, 16 * (NX * (CAP0 + C1) // P))
            pool.wait_ge(s_idx, 1)
            for t in range(NT):
                for k in range(2):
                    scatter(k, t, disp0_d, s_disp)
            pool.wait_ge(s_es, 48 * NX)
            for n in range(2 * NT):
                gather(n, n % 2, n // 2, eout0_d, 0)
            pool.wait_ge(s_idx, 2)
            for t in range(NT):
                scatter(0, t, disp1_d, s_disp1)
            for stored in (s_fs0, s_fs1):
                pool.wait_ge(stored, 16 * NX // 2)
            for n in range(NT):
                gather(n, 0, n, eout1_d, 2 * NT)

        @block.tensor
        def _(pe):
            def group(o_, pairs, s):
                for j, (l, r) in enumerate(pairs):
                    mm = pe.matmul(o_, l, r, start=(j == 0), stop=(j == len(pairs) - 1))
                mm.then_inc(s, 1)

            pe.wait_ge(s_const, 5)
            pe.wait_ge(s_cnt, 1)
            group(bank(0, NBK), [(before[:, :], bk[:, 2, 0:NBK])], s_tot)
            group(bank(1, NBK), [(ones[:, :], bk[:, 2, 0:NBK])], s_tot)
            pe.wait_ge(s_ln, NT)
            for g in range(2 * KD):
                k, hf = g // 2, g % 2
                if g >= 4:
                    pe.wait_ge(s_xt_ev, g - 3)
                for t in range(4):
                    mm = pe.transpose(psum[:, 4 + g % 4, t * P:(t + 1) * P], XL[:, 4 * hf + t, k * P:(k + 1) * P], ident[:, :])
                mm.then_inc(s_xt_mm, 1)

            def pair(c, par, reuse):
                pe.wait_ge(s_hot, c + 1)
                if reuse:
                    pe.wait_ge(s_added, c - 1)
                for h in range(2):
                    mm = pe.matmul(bank(2 * par + h), S1[:, par, :], D1[:, par, 512 * h:512 * h + 512], start=True, stop=True)
                mm.then_inc(s_pair, 1)
            pair(0, 0, False)
            pair(1, 1, False)
            with pe.Fori(1, NCH // 2) as i:
                pair(i * 2, 0, True)
                pair(i * 2 + 1, 1, True)
            pe.wait_ge(s_mn, 1)
            pe.wait_ge(s_added, NCH)
            for j in range(NT):
                if j >= 4:
                    pe.wait_ge(s_mk_ev, j - 3)
                for t in range(NT):
                    mm = pe.transpose(psum[:, j % 4, :].bitcast(bf16)[:, t * P:(t + 1) * P], MN[:, t, j * P:(j + 1) * P], identb[:, :])
                mm.then_inc(s_mk_mm, 1)
            pe.wait_ge(s_mk_ev, NT)
            pe.wait_ge(s_xt_ev, 12)

            def h_groups(i):
                pe.wait_ge(s_w1, i * 16 + 16)
                for g in range(16):
                    hf, t = g // NT, g % NT
                    if g >= 4:
                        pe.wait_ge(s_h_ev, i * 16 + (g - 3))
                    group(bank(g % 4, HD), [(XT[:, k, t * P:(t + 1) * P], W1[:, k, hf * HD:(hf + 1) * HD]) for k in range(KD)], s_h_mm)

            def proj_groups(i, gs):
                for g in gs:
                    hf, t = g // NT, g % NT
                    if g == 0:
                        pe.wait_ge(s_w2, i * 16 + 16)
                        pe.wait_ge(s_ot, i * 12 + 12)
                    if g >= 4:
                        pe.wait_ge(s_acc_ev, i * 16 + (g - 3))
                    group(bank(4 + g % 4, HD), [(OT[:, k, t * P:(t + 1) * P], W2[:, k, hf * HD:(hf + 1) * HD]) for k in range(KD)], s_p_mm)

            def rows_bc(i, ks, value):
                pe.wait_ge(s_diag, i * 2 + value)
                for n, k in enumerate(ks):
                    for hf in range(2):
                        mm = pe.matmul(bank(2 * n + hf), ones[:, :], diag[:, k, hf * 512:(hf + 1) * 512], start=True, stop=True)
                mm.then_inc(s_bc, 1)

            def head(i, first=False):
                h_groups(i)
                if not first:
                    proj_groups(i - 1, range(0, 4))
                rows_bc(i, (0, 1), 1)
                if not first:
                    proj_groups(i - 1, range(4, 10))
                rows_bc(i, (2,), 2)
                if not first:
                    proj_groups(i - 1, range(10, 16))
                    pe.wait_ge(s_acc_ev, i * 16)
                for g in range(14):
                    hf, f = g // 7, g % 7 - 1
                    if g % 7 == 0:
                        pe.wait_ge(s_P, i * 2 + hf + 1)
                    if g >= 4:
                        pe.wait_ge(s_agg_ev, i * 14 + (g - 3))
                    d = slice(hf * NH, (hf + 1) * NH)
                    group(bank(4 + g % 4), [(ones[:, :] if f < 0 else H[:, s, f * P:(f + 1) * P], PM[:, s, d]) for s in range(NT)], s_agg_mm)

            head(0, True)
            with pe.Fori(1, H1) as i:
                head(i)
            proj_groups(H1 - 1, range(16))
            rows_bc(H1, (0, 1), 1)
            rows_bc(H1, (2,), 2)
            pe.wait_ge(s_P, H1 * 2 + 2)
            pe.wait_ge(s_acc_ev, H1 * 16)
            for t in range(NT):
                for s in range(NT):
                    mm = pe.matmul(psum[:, 0, t:t + 1], PM[:, s, t * P:(t + 1) * P], ones[:, 0:1], start=(s == 0), stop=(s == NT - 1))
            mm.then_inc(s_g2_mm, 1)
            for g in range(16):
                t, hf = g // 2, g % 2
                if g >= 4:
                    pe.wait_ge(s_x1, g - 3)
                group(bank(4 + g % 4, HD), [(PM[:, s, t * P:(t + 1) * P], ACC[:, s, hf * HD:(hf + 1) * HD]) for s in range(NT)], s_g2_mm)

            def turn_rows(n):
                pe.wait_ge(s_ln, NT * (2 * n + 2))
                for g in range(2 * KD):
                    k, hf = g // 2, g % 2
                    if g >= 4:
                        pe.wait_ge(s_xt_ev, 12 * (n + 1) + g - 3)
                    for t in range(4):
                        mm = pe.transpose(psum[:, 4 + g % 4, t * P:(t + 1) * P], LN[:, 4 * hf + t, k * P:(k + 1) * P], ident[:, :])
                    mm.then_inc(s_xt_mm, 1)

            def logits(n):
                pe.wait_ge(s_xt_ev, 12 * (n + 2))
                pe.wait_ge(s_wr, 16 * (n + 1))
                for t in range(NT):
                    for k in range(KD):
                        mm = pe.matmul(psum[:, 0, t * NX:(t + 1) * NX], LT[:, k, t * P:(t + 1) * P], Wr[:, k, :], start=(k == 0), stop=(k == KD - 1))
                mm.then_inc(s_lg, 1)

            turn_rows(0)
            logits(0)
            pe.wait_ge(s_sw, 48)

            def shared_up(j):
                m, hf = j // 2, j % 2
                if j >= 2:
                    pe.wait_ge(s_sact, j - 1)
                for n in range(2):
                    for k in range(KD):
                        mm = pe.matmul(bank(4 + 2 * (j % 2) + n), SW[n][:, k, m * P:(m + 1) * P], LT[:, k, hf * NH:(hf + 1) * NH], start=(k == 0), stop=(k == KD - 1))
                mm.then_inc(s_sg_mm, 1)
            for j in range(6):
                shared_up(j)
            pe.wait_ge(s_rt_in, 1)
            for j in range(3):
                for t in range(NT):
                    src_ = (rt[:, 4, t, :], rt[:, 2, t, :], rt[:, 3, t, :])[j]
                    mm = pe.transpose(psum[0:NX, (0, 2, 0)[j] + t // 4, (t % 4) * P:(t % 4 + 1) * P], src_, ident[:, :])
                    if j == 1 and t == NT - 1:
                        mm.then_inc(s_rt_mm, 1)
                        pe.wait_ge(s_rt_ev, 1)
            mm.then_inc(s_rt_mm, 1)
            pe.wait_ge(s_rt_ev, 3)
            pe.wait_ge(s_sact, 6)
            for n in range(2 * NT):
                t, k = n // 2, n % 2
                if n >= 2:
                    pe.wait_ge(s_rank, n - 1)
                for hf in range(2):
                    mm = pe.matmul(bank(2 * (n % 2) + hf), rowsT[0:NX, 1 + k, t * P:(t + 1) * P], rowsT[0:NX, 0, hf * 512:(hf + 1) * 512], start=True, stop=True)
                mm.then_inc(s_rr_mm, 1)
                t, hf = n // 2, n % 2
                if n >= 4:
                    pe.wait_ge(s_so_ev, n - 3)
                group(bank(4 + n % 4, HD), [(SA[:, m, t * P:(t + 1) * P], SW[2][:, m, hf * HD:(hf + 1) * HD]) for m in range(KM)], s_so_mm)
            pe.wait_ge(s_so_ev, 16)
            pe.wait_ge(s_rank, 16)
            s_ew, s_dr = (s_ew0, s_ew1), (s_dr0, s_dr1)

            def expert(e, i, b, reuse):
                w1, w3, w2 = EW[b]
                pe.wait_ge(s_dr[b], i * 48 + 48)
                for k in range(KD):
                    if k >= 2 or reuse:
                        pe.wait_ge(s_dt_ev, e * 6 + (k - 1))
                    for j, (c0, cn) in enumerate(CB0):
                        mm = pe.transpose(psum[:, k % 2, c0:c0 + cn], DR[b][0:cn, j, k * P:(k + 1) * P], ident[0:cn, 0:cn])
                    mm.then_inc(s_dt_mm, 1)
                pe.wait_ge(s_dt_ev, e * 6 + 6)
                pe.wait_ge(s_ew[b], i * 48 + 48)
                for m in range(KM):
                    if m >= 2 or reuse:
                        pe.wait_ge(s_act, e * 3 + (m - 1))
                    for n, w in enumerate((w1, w3)):
                        for k in range(KD):
                            mm = pe.matmul(bank(2 + 2 * (m % 2) + n, CAP0), w[:, k, m * P:(m + 1) * P], DT[:, k, :], start=(k == 0), stop=(k == KD - 1))
                    mm.then_inc(s_gu_mm, 1)
                pe.wait_ge(s_act, e * 3 + 3)
                for j, (c0, cn) in enumerate(CB0):
                    for hf in range(2):
                        g = 2 * j + hf
                        if g >= 2 or reuse:
                            pe.wait_ge(s_eo_ev, e * 6 + (g - 1))
                        group(psum[0:cn, 6 + hf, 0:HD], [(EA[:, m, c0:c0 + cn], w2[:, m, hf * HD:(hf + 1) * HD]) for m in range(KM)], s_eo_mm)
            expert(0, 0, 0, False)
            expert(1, 0, 1, True)
            with pe.Fori(1, NX // 2) as i:
                expert(i * 2, i, 0, True)
                expert(i * 2 + 1, i, 1, True)

            y0 = z0 = 0
            for lay in range(3):
                ft, fo = RIN[lay] // P, ROUT[lay]
                w_, h_ = cut(RW, [ft, fo]), cut(HN, [NT, RIN[lay]])
                fh = fo // 2
                pe.wait_ge(s_hn, 1) if lay == 0 else pe.wait_ge(s_relu, 16 * lay)
                for g in range(2 * ft):
                    f, hf = g // 2, g % 2
                    if g >= 4 or lay:
                        pe.wait_ge(s_y_ev, y0 + g - 3)
                    for t in range(4):
                        mm = pe.transpose(psum[:, g % 4, t * P:(t + 1) * P], h_[:, 4 * hf + t, f * P:(f + 1) * P], ident[:, :])
                    mm.then_inc(s_y_mm, 1)

                def project(w, yn, zn):
                    pe.wait_ge(s_rw, w * 16 + 16)
                    pe.wait_ge(s_y_ev, yn)
                    for g in range(16):
                        t, hf = g // 2, g % 2
                        if g >= 4 or not isinstance(zn, int) or zn:
                            pe.wait_ge(s_z_ev, zn + (g - 3))
                        group(bank(4 + g % 4, fh), [(YT[:, k, t * P:(t + 1) * P], w_[:, k, hf * fh:(hf + 1) * fh]) for k in range(ft)], s_z_mm)
                project(4 * lay, y0 + 2 * ft, z0)
                extra = 2 if lay == 0 else 0
                per = 2 * ft + extra
                with pe.Fori(0, R) as r:
                    pe.wait_ge(s_af, r + (lay * R + 1))
                    yb = r * per + (y0 + 2 * ft)
                    for g in range(per):
                        pe.wait_ge(s_y_ev, yb + (g - 3))
                        n = g - extra
                        f, hf = n // 2, g % 2
                        group(bank(g % 4), [(ones[:, :] if n < 0 else h_[:, s, f * P:(f + 1) * P], AF[:, s, hf * NH:(hf + 1) * NH]) for s in range(NT)], s_y_mm)
                    project(r + (4 * lay + 1), yb + per, r * 16 + (z0 + 16))
                y0 += 2 * ft + R * per
                z0 += 64

            turn_rows(1)
            logits(1)
            pe.wait_ge(s_rt_in, 2)
            for t in range(NT):
                for j in range(t + 1):
                    mm = pe.matmul(psum[:, 0, t * NX:(t + 1) * NX], ones[:, :] if j < t else before[:, :], rt[:, 2, j, :], start=(j == 0), stop=(j == t))
            mm.then_inc(s_rr_mm, 1)
            s_fw, s_fr = (s_fw0, s_fw1), (s_fr0, s_fr1)
            pe.wait_ge(s_idx, 2)

            def expert1(e, i, b, reuse):
                w1, w2 = GW[b]
                pe.wait_ge(s_fr[b], i * 16 + 16)
                for j in range(2):
                    if reuse:
                        pe.wait_ge(s_ft_ev, e * 2 + (j - 1))
                    for k in range(3):
                        mm = pe.transpose(psum[:, j, k * P:(k + 1) * P], GD[b][:, (3 * j + k) * P:(3 * j + k + 1) * P], ident[:, :])
                    mm.then_inc(s_ft_mm, 1)
                pe.wait_ge(s_ft_ev, e * 2 + 2)
                pe.wait_ge(s_fw[b], i * 64 + 64)
                for m in range(KM):
                    if reuse:
                        pe.wait_ge(s_f1, e * 3 + (m - 2))
                    group(bank(2 + m, C1), [(w1[:, k, m * P:(m + 1) * P], GT[:, k, :]) for k in range(KD)], s_f1_mm)
                pe.wait_ge(s_f1, e * 3 + 3)
                for hf in range(2):
                    if reuse:
                        pe.wait_ge(s_f3, e * 2 + (hf - 1))
                    group(bank(6 + hf, HD), [(GA[:, m, :], w2[:, m, hf * HD:(hf + 1) * HD]) for m in range(KM)], s_f2_mm)
            expert1(0, 0, 0, False)
            expert1(1, 0, 1, True)
            with pe.Fori(1, NX // 2) as i:
                expert1(i * 2, i, 0, True)
                expert1(i * 2 + 1, i, 1, True)

        @block.scalar
        def _(act):
            ch = Chain(act, ach)
            act.wait_ge(s_var, 1)
            act.activation(rstd[:, :], rstd[:, :], ACT.Sqrt).then_inc(s_std, 1)
            for g in range(2 * KD):
                k, hf = g // 2, g % 2
                act.wait_ge(s_xt_mm, g + 1)
                if g == 0:
                    act.wait_ge(s_zero, 16 * (NX * (CAP0 + C1) // P))
                act.activation(XT[:, k, hf * NH:(hf + 1) * NH], bank(4 + g % 4), ACT.Copy).then_inc(s_xt_ev, 1)
            for j in range(NT):
                act.wait_ge(s_mk_mm, j + 1)
                act.activation(MK[:, j, :], psum[:, j % 4, :].bitcast(bf16), ACT.Copy).then_inc(s_mk_ev, 1)

            def probs(i):
                act.wait_ge(s_rows, i + 1)
                for n in range(2 * NT):
                    hf, s = n // NT, n % NT
                    if n >= 2:
                        act.wait_ge(s_larger, i * 16 + (n - 1))
                    act.activation(ET[:, n % 2, :], bank(2 + hf), ACT.Exp, bias=alpha_low[:, s:s + 1])
                    act.activation(PM[:, s, hf * NH:(hf + 1) * NH], bank(hf), ACT.Exp, bias=alpha[:, 0, s:s + 1]).then_inc(s_exp, 1)

            def head(i, first=False):
                for g in range(16):
                    hf, t = g // NT, g % NT
                    act.wait_ge(s_h_mm, i * 16 + g + 1)
                    act.activation(H[:, t, hf * HD:(hf + 1) * HD], bank(g % 4, HD), ACT.Copy).then_inc(s_h_ev, 1)
                probs(i)
                act.wait_ge(s_b1, i * 16 + 16)
                for g in range(2 * KD):
                    hf, f = g // KD, g % KD
                    o_ = OT[:, f, hf * NH:(hf + 1) * NH]
                    act.wait_ge(s_agg_ev, i * 14 + hf * 7 + f + 2)
                    if g >= 2:
                        act.wait_ge(s_ot, i * 12 + (g - 1))
                    ch.step(act.activation(ET[:, g % 2, :], o_, ACT.Exp, bias=b1c[:, f:f + 1]))
                    ch.sync()
                    act.activation(o_, o_, ACT.Relu, bias=b1c[:, f:f + 1]).then_inc(s_elu, 1)

            head(0, True)
            with act.Fori(1, H1) as i:
                ch.turn(i, 1, 12)
                head(i)
            ch.leave(H1 - 1, 12)
            probs(H1)

            def root_of_variance(n):
                act.wait_ge(s_var, n + 1)
                act.activation(rstd[:, :], rstd[:, :], ACT.Sqrt).then_inc(s_std, 1)

            def turned_rows(n):
                root_of_variance(n + 1)
                for g in range(2 * KD):
                    k, hf = g // 2, g % 2
                    act.wait_ge(s_xt_mm, 12 * (n + 1) + g + 1)
                    act.activation(LT[:, k, hf * NH:(hf + 1) * NH], bank(4 + g % 4), ACT.Copy).then_inc(s_xt_ev, 1)

            def router_exp(n):
                act.wait_ge(s_ct, n + 1)
                act.activation(rt[:, 0], rt[:, 0], ACT.Exp).then_inc(s_exps, 1)

            turned_rows(0)
            router_exp(0)
            for j in range(6):
                act.wait_ge(s_sg_mm, j + 1)
                if j >= 2:
                    act.wait_ge(s_sact, j - 1)
                act.activation(SG[:, j % 2, :], bank(4 + 2 * (j % 2)), ACT.Silu).then_inc(s_ssilu, 1)
            for j in range(3):
                act.wait_ge(s_rt_mm, 1 + j // 2)
                b0 = 2 * j if j < 2 else 0
                act.activation(rowsT[0:NX, j, :], psum[0:NX, b0:b0 + 2, :].rearrange("p a b -> p (a b)"), ACT.Copy).then_inc(s_rt_ev, 1)

            def expert(e, reuse):
                for k in range(KD):
                    act.wait_ge(s_dt_mm, e * 6 + (k + 1))
                    act.activation(DT[:, k, :], bank(k % 2, CAP0), ACT.Copy).then_inc(s_dt_ev, 1)
                for m in range(KM):
                    act.wait_ge(s_gu_mm, e * 3 + (m + 1))
                    if m >= 2 or reuse:
                        act.wait_ge(s_act, e * 3 + (m - 1))
                    act.activation(EG[:, m % 2, :], bank(2 + 2 * (m % 2), CAP0), ACT.Silu).then_inc(s_silu, 1)
                for j, (c0, cn) in enumerate(CB0):
                    for hf in range(2):
                        g = 2 * j + hf
                        act.wait_ge(s_eo_mm, e * 6 + (g + 1))
                        if reuse and g == 0:
                            act.wait_ge(s_es, e * 48)
                        act.activation(EO[0:cn, j, hf * HD:(hf + 1) * HD], psum[0:cn, 6 + hf, 0:HD], ACT.Copy).then_inc(s_eo_ev, 1)
                    act.wait_ge(s_eo_ev, e * 6 + (2 * j + 2))
                    act.dma_start(eout0_d[bass.ds(e * CAP0 + c0, cn), :], EO[0:cn, j, :]).then_inc(s_es, 16)
            expert(0, False)
            with act.Fori(1, NX) as e:
                expert(e, True)

            root_of_variance(2)
            y0 = 0
            for lay in range(3):
                ft, fo = RIN[lay] // P, ROUT[lay]
                fh = fo // 2
                for g in range(2 * ft):
                    f, hf = g // 2, g % 2
                    act.wait_ge(s_y_mm, y0 + g + 1)
                    act.activation(YT[:, f, hf * NH:(hf + 1) * NH], bank(g % 4), ACT.Copy).then_inc(s_y_ev, 1)
                per = 2 * ft + (2 if lay == 0 else 0)

                def widen(n, yn):
                    act.wait_ge(s_ar, n * 16 + 16)
                    act.wait_ge(s_y_mm, yn)
                    act.activation(AF.rearrange("p a b -> p (a b)"), AR, ACT.Copy).then_inc(s_af, 1)
                with act.Fori(0, R) as r:
                    widen(r + lay * R, r * per + (y0 + 2 * ft))
                y0 += 2 * ft + R * per
                if lay < 2:
                    o_ = cut(HN, [NT, fo])
                    for g in range(16):
                        t, hf = g // 2, g % 2
                        act.wait_ge(s_z_ev, 64 * lay + 48 + g + 1)
                        act.activation(o_[:, t, hf * fh:(hf + 1) * fh], cut(13312, [NT, fo])[:, t, hf * fh:(hf + 1) * fh], ACT.Relu).then_inc(s_relu, 1)

            root_of_variance(3)
            for g in range(2 * KD):
                k, hf = g // 2, g % 2
                act.wait_ge(s_xt_mm, 24 + g + 1)
                act.activation(LT[:, k, hf * NH:(hf + 1) * NH], bank(4 + g % 4), ACT.Copy).then_inc(s_xt_ev, 1)
            router_exp(1)
            s_fw = (s_fw0, s_fw1)

            def expert1(e, i, b, reuse):
                for j in range(2):
                    act.wait_ge(s_ft_mm, e * 2 + (j + 1))
                    act.activation(GT[:, 3 * j:3 * j + 3, :].rearrange("p a b -> p (a b)"), bank(j, 3 * P), ACT.Copy).then_inc(s_ft_ev, 1)
                act.wait_ge(s_fw[b], i * 64 + 64)
                for m in range(KM):
                    act.wait_ge(s_f1_mm, e * 3 + (m + 1))
                    act.activation(GA[:, m, :], bank(2 + m, C1), ACT.Gelu_apprx_tanh, bias=gb1[b][:, m:m + 1]).then_inc(s_f1, 1)
                for hf in range(2):
                    act.wait_ge(s_f3, e * 2 + (hf + 1))
                    g_ = GO[:, b, hf * HD:(hf + 1) * HD]
                    act.activation(g_, g_, ACT.Gelu_apprx_tanh).then_inc(s_f2, 1)
                act.wait_ge(s_f2, e * 2 + 2)
                act.dma_start(eout1_d[bass.ds(e * C1, C1), :], GO[:, b, :]).then_inc((s_fs0, s_fs1)[b], 16)
            expert1(0, 0, 0, False)
            expert1(1, 0, 1, True)
            with act.Fori(1, NX // 2) as i:
                expert1(i * 2, i, 0, True)
                expert1(i * 2 + 1, i, 1, True)

        @block.vector
        def _(dve):
            ch = Chain(dve, dch)
            step, sync = ch.step, ch.sync

            def norm_stats(xv, t):
                for h in range(2):
                    step(dve.bn_stats(stats[:, t, h, :], xv[:, t, h * HD:(h + 1) * HD]))
                sync()
                step(dve.bn_aggr(mv[:, t, :], stats[:, t, :, :]))

            def normalize(xv, o_):
                for t in range(NT):
                    norm_stats(xv, t)
                sync()
                dve.tensor_scalar(rstd[:, :], mv[:, :, 1], EPS, None, ADD).then_inc(s_var, 1)

            dve.wait_ge(s_edges, 48)
            e_src, e_dst, e_typ = (edges[:, k, :] for k in range(3))
            step(dve.tensor_scalar(ework[:, 0, :], e_src, 7, None, ALU.logical_shift_right))
            step(dve.tensor_scalar(ework[:, 1, :], e_src, P - 1, 10, ALU.bitwise_and, ALU.logical_shift_left))
            step(dve.tensor_scalar(ework[:, 3, :], e_typ, 3, None, ALU.logical_shift_left))
            sync()
            step(dve.tensor_tensor(ework[:, 2, :], ework[:, 1, :], e_dst, ALU.bitwise_or))
            step(dve.tensor_tensor(ework[:, 4, :], ework[:, 3, :], ework[:, 0, :], ALU.bitwise_or))
            sync()
            step(dve.tensor_copy(keyf, ework[:, 4, :]))
            sync()
            dve.wait_ge(s_const, 5)
            step(dve.tensor_tensor(onehot, keyf.unsqueeze(1).to_broadcast([P, NBK, EC]),
                                   iota[:, 0:NBK].unsqueeze(2).to_broadcast([P, NBK, EC]), ALU.is_equal))
            step(dve.memset(bk[:, 0, 0:1], 0.0))
            sync()
            step(dve.tensor_tensor_scan(running.rearrange("p b c -> p (b c)"),
                                        ones[:, 0:1].to_broadcast([P, NBK * EC]),
                                        onehot.rearrange("p b c -> p (b c)"), 0.0, MULT, ADD))
            sync()
            step(dve.tensor_copy(bk[:, 0, 1:NBK + 1], running[:, :, EC - 1]))
            sync()
            dve.tensor_tensor(bk[:, 2, 0:NBK], bk[:, 0, 1:NBK + 1], bk[:, 0, 0:NBK], SUB).then_inc(s_cnt, 1)
            dve.wait_ge(s_tot, 2)
            step(dve.tensor_scalar(bki, bank(1, NBK), float(P - 1), None, ADD))
            sync()
            step(dve.tensor_scalar(bki, bki, 7, None, ALU.logical_shift_right))
            sync()
            step(dve.tensor_copy(bk[:, 3, 0:NBK], bki))
            sync()
            step(dve.tensor_tensor_scan(bk[:, 4, 0:NBK], ones[:, 0:1].to_broadcast([P, NBK]), bk[:, 3, 0:NBK], 0.0, MULT, ADD))
            step(dve.tensor_tensor(bk[:, 5, 0:NBK], bank(0, NBK), bk[:, 0, 0:NBK], SUB))
            sync()
            step(dve.tensor_tensor(bk[:, 6, 0:NBK], bk[:, 4, 0:NBK], bk[:, 3, 0:NBK], SUB))
            sync()
            step(dve.scalar_tensor_tensor(bk[:, 7, 0:NBK], bk[:, 6, 0:NBK], float(P), bk[:, 5, 0:NBK], MULT, ADD))
            sync()
            step(dve.tensor_scalar(bk[:, 8, 0:NBK], bk[:, 7, 0:NBK], -1.0, None, ADD))
            sync()
            step(dve.tensor_tensor(running, running, bk[:, 8, 0:NBK].unsqueeze(2).to_broadcast([P, NBK, EC]), ADD))
            sync()
            step(dve.tensor_tensor(running, running, onehot, MULT))
            sync()
            step(dve.tensor_reduce(slotf, running.rearrange("p b c -> p c b"), AX.X, ADD))
            sync()
            step(dve.tensor_copy(sloti[:, 0, :], slotf))
            sync()
            step(dve.tensor_scalar(sloti[:, 1, :], sloti[:, 0, :], 7, None, ALU.logical_shift_right))
            step(dve.tensor_scalar(sloti[:, 2, :], sloti[:, 0, :], P - 1, None, ALU.bitwise_and))
            sync()
            dve.scalar_tensor_tensor(row, sloti[:, 2, :], float(NCH), sloti[:, 1, :], MULT, ADD).then_inc(s_row, 1)
            step(dve.tensor_tensor(cmp[0:1], iota[0:1, 0:NCH].unsqueeze(2).to_broadcast([1, NCH, NBK]),
                                   bk[0:1, 4, 0:NBK].unsqueeze(1).to_broadcast([1, NCH, NBK]), ALU.is_ge))
            sync()
            step(dve.tensor_reduce(boff[0:1], cmp[0:1], AX.X, ADD))
            sync()
            step(dve.tensor_scalar(boffi[0:1], boff[0:1], float(NBK - 1), float(N), MIN, MULT))
            step(dve.tensor_copy(iotah, iota))
            step(dve.tensor_copy(identb[:, :], ident[:, :]))
            dve.wait_ge(s_x, 16)
            normalize(XL, XL)
            dve.wait_ge(s_std, 1)
            step(dve.reciprocal(rstd[:, :], rstd[:, :]))
            sync()
            for t in range(NT):
                dve.tensor_scalar(XL[:, t, :], XL[:, t, :], mv[:, t, 0:1], rstd[:, t:t + 1], SUB, MULT).then_inc(s_ln, 1)
            dve.wait_ge(s_recs, 16)
            step(dve.tensor_scalar(recs[:, 1, :], recs[:, 0, :], 10, None, ALU.arith_shift_right))
            step(dve.tensor_scalar(recs[:, 2, :], recs[:, 0, :], N - 1, None, ALU.bitwise_and))
            sync()
            step(dve.tensor_copy(recf, recs[:, 1:3, :]))
            sync()
            dve.wait_ge(s_azero, 1)

            def hots(c, par, reuse):
                if reuse:
                    dve.wait_ge(s_pair, c - 1)
                dve.tensor_scalar(S1[:, par, :], iotah[:, 0:P], recf[:, 0, bass.ds(c, 1)], None, ALU.is_equal)
                dve.tensor_scalar(D1[:, par, :], iotah, recf[:, 1, bass.ds(c, 1)], None, ALU.is_equal).then_inc(s_hot, 1)

            def add(c, par, first=False):
                off = dve.value_load(boffi[0:1, bass.ds(c, 1)], min_val=0, max_val=(NBK - 1) * N)
                dve.wait_ge(s_pair, c + 1)
                if not first:
                    dve.wait_ge(s_added, c)
                part = A_r[:, bass.ds(off, N)]
                dve.tensor_tensor(part, psum[:, 2 * par:2 * par + 2, :].rearrange("p a b -> p (a b)"), part, ADD).then_inc(s_added, 1)
            hots(0, 0, False)
            hots(1, 1, False)
            add(0, 0, True)
            with dve.Fori(0, NCH // 2 - 1) as i:
                hots(i * 2 + 2, 0, True)
                add(i * 2 + 1, 1)
                hots(i * 2 + 3, 1, True)
                add(i * 2 + 2, 0)
            add(NCH - 1, 1)
            dve.wait_ge(s_added, NCH)
            ATf = AT.rearrange("p a b -> p (a b)")
            step(dve.tensor_tensor(ATf, A_r[:, 0:NT * N], A_r[:, NT * N:2 * NT * N], ADD))
            sync()
            step(dve.tensor_tensor(ATf, ATf, A_r[:, 2 * NT * N:3 * NT * N], ADD))
            sync()
            dve.tensor_scalar(MN.rearrange("p a b -> p (a b)"), ATf, 0.0, NEG, ALU.is_equal, MULT).then_inc(s_mn, 1)
            dve.tensor_copy(mx[:, 3, 0:1], ones[:, 0:1]).then_inc(s_at, 1)

            def acc_evac(i, gs, first):
                for g in gs:
                    hf, t = g // NT, g % NT
                    a_ = ACC[:, t, hf * HD:(hf + 1) * HD]
                    dve.wait_ge(s_p_mm, i * 16 + g + 1)
                    if first:
                        dve.tensor_copy(a_, bank(4 + g % 4, HD)).then_inc(s_acc_ev, 1)
                    else:
                        dve.tensor_tensor(a_, bank(4 + g % 4, HD), a_, ADD).then_inc(s_acc_ev, 1)

            def attention(i, hv, evac):
                dve.wait_ge(s_a, i * 32 + 32)
                for k in range(2):
                    for t in range(NT):
                        step(dve.tensor_tensor_reduce(junk[:, 0:D], hv[:, t, :], a_bc[:, k, :], 1.0, 0.0, MULT, ADD, alpha[:, k, t:t + 1]))
                        sync()
                for k in range(2):
                    ins = dve.tensor_tensor(diag[:, k, :].rearrange("p (t n) -> p t n", t=NT),
                                            ident[:, :].unsqueeze(1).to_broadcast([P, NT, P]),
                                            alpha[:, k, :].unsqueeze(2).to_broadcast([P, NT, P]), MULT)
                ins.then_inc(s_diag, 1)
                evac(range(0, 4))
                dve.wait_ge(s_bc, i * 2 + 1)
                srow = psum[:, 0:2, :].rearrange("p a b -> p (a b)")
                for t in range(NT):
                    step(dve.tensor_copy(mx[:, 3, t:t + 1], ones[:, 0:1]))
                    step(dve.tensor_tensor_reduce(junk, MK[:, t, :], srow, 1.0, 3 * NEG, ADD, MAX, mx[:, 0, t:t + 1]))
                    sync()
                step(dve.tensor_tensor(mx[:, 1, :], mx[:, 0, :], alpha[:, 1, :], ADD))
                sync()
                step(dve.scalar_tensor_tensor(mx[:, 2, :], mx[:, 1, :], 0.2, mx[:, 1, :], MULT, MAX))
                sync()
                dve.tensor_tensor(diag[:, 2, :].rearrange("p (t n) -> p t n", t=NT),
                                  ident[:, :].unsqueeze(1).to_broadcast([P, NT, P]),
                                  mx[:, 2, :].unsqueeze(2).to_broadcast([P, NT, P]), MULT).then_inc(s_diag, 1)
                evac(range(4, 10))
                dve.wait_ge(s_bc, i * 2 + 2)
                step(dve.tensor_copy(junk, srow))
                step(dve.tensor_scalar(alpha_low[:, :], alpha[:, 0, :], 0.2, None, MULT))
                sync()
                drow = psum[:, 2:4, :].rearrange("p a b -> p (a b)")
                step(dve.tensor_tensor(srow, drow, junk, SUB))
                sync()
                dve.scalar_tensor_tensor(drow, drow, 0.2, junk, MULT, SUB).then_inc(s_rows, 1)
                evac(range(10, 16))
                for n in range(2 * NT):
                    hf, s = n // NT, n % NT
                    p_ = PM[:, s, hf * NH:(hf + 1) * NH]
                    dve.wait_ge(s_exp, i * 16 + n + 1)
                    dve.scalar_tensor_tensor(p_, p_, 1.0, ET[:, n % 2, :], MIN, MAX).then_inc(s_larger, 1)
                    if s == NT - 1:
                        d = slice(hf * NH, (hf + 1) * NH)
                        dve.wait_ge(s_larger, i * 16 + n + 1)
                        dve.scalar_tensor_tensor(PM[:, :, d], PM[:, :, d], 1.0, AT[:, :, d], MIN, MULT).then_inc(s_P, 1)

            def head(i, first=False, second=False):
                dve.wait_ge(s_h_ev, i * 16 + 16)
                attention(i, H, lambda gs: None if first else acc_evac(i - 1, gs, second))

                def fix(g):
                    dve.wait_ge(s_elu, i * 12 + g + 1)
                    dve.tensor_scalar(ET[:, g % 2, :], ET[:, g % 2, :], 1.0, -1.0, MIN, ADD).then_inc(s_efix, 1)
                for hf in range(2):
                    dve.wait_ge(s_agg_mm, i * 14 + hf * 7 + 1)
                    if hf or not first:
                        dve.wait_ge(s_agg_ev, i * 14 + hf * 7)
                    step(dve.tensor_scalar(RD, bank(4 + (hf * 7) % 4), 1e-16, None, ADD))
                    sync()
                    dve.reciprocal(RD, RD).then_inc(s_agg_ev, 1)
                    for f in range(KD):
                        g = hf * 7 + 1 + f
                        dve.wait_ge(s_agg_mm, i * 14 + g + 1)
                        dve.wait_ge(s_agg_ev, i * 14 + hf * 7 + 1)
                        dve.tensor_tensor(OT[:, f, hf * NH:(hf + 1) * NH], bank(4 + g % 4), RD, MULT).then_inc(s_agg_ev, 1)
                        n = hf * KD + f
                        if n >= 1:
                            fix(n - 1)
                fix(2 * KD - 1)

            head(0, first=True)
            head(1, second=True)
            PER = 16 + 16 + 2 + 3 + 2
            with dve.Fori(2, H1) as i:
                ch.turn(i, 2, PER)
                head(i)
            ch.leave(H1 - 2, PER)
            acc_evac(H1 - 1, range(16), False)
            dve.wait_ge(s_acc_ev, H1 * 16)
            attention(H1, ACC, lambda gs: None)
            dve.wait_ge(s_g2_mm, 1)
            step(dve.tensor_scalar(rd2[:, :], psum[:, 0, 0:NT], 1e-16, None, ADD))
            sync()
            step(dve.reciprocal(rd2[:, :], rd2[:, :]))
            sync()
            dve.wait_ge(s_xr, 32)
            for t in range(NT):
                step(dve.tensor_tensor(XN[:, t, :], XN[:, t, :], b2_bc, ADD))
            sync()
            for g in range(16):
                t, hf = g // 2, g % 2
                x_ = XN[:, t, hf * HD:(hf + 1) * HD]
                dve.wait_ge(s_g2_mm, g + 2)
                dve.scalar_tensor_tensor(x_, bank(4 + g % 4, HD), rd2[:, t:t + 1], x_, MULT, ADD).then_inc(s_x1, 1)

            def layernorm(n, to, width):
                sync()
                for t in range(NT):
                    norm_stats(XN, t)
                sync()
                dve.wait_ge(s_ln, NT * n)
                dve.tensor_scalar(rstd[:, :], mv[:, :, 1], EPS, None, ADD).then_inc(s_var, 1)
                dve.wait_ge(s_std, n + 1)
                step(dve.reciprocal(rstd[:, :], rstd[:, :]))
                sync()
                for t in range(NT):
                    dve.tensor_scalar(to[:, t, 0:D], XN[:, t, :], mv[:, t, 0:1], rstd[:, t:t + 1], SUB, MULT).then_inc(s_ln, 1)

            def over_experts(v):
                return v.unsqueeze(2).to_broadcast([P, NT, NX])

            def router_probs(n):
                dve.wait_ge(s_lg, n + 1)
                step(dve.tensor_copy(rt[:, 0], psum[:, 0, 0:NT * NX].rearrange("p (a b) -> p a b", a=NT)))
                sync()
                step(dve.tensor_reduce(rk[:, 0, 0], rt[:, 0], AX.X, MAX))
                sync()
                dve.tensor_tensor(rt[:, 0], rt[:, 0], over_experts(rk[:, 0, 0]), SUB).then_inc(s_ct, 1)
                dve.wait_ge(s_exps, n + 1)
                step(dve.tensor_reduce(rk[:, 0, 1], rt[:, 0], AX.X, ADD))
                sync()
                step(dve.reciprocal(rk[:, 0, 1], rk[:, 0, 1]))
                sync()
                step(dve.tensor_tensor(rt[:, 1], rt[:, 0], over_experts(rk[:, 0, 1]), MULT))
                sync()
                for t in range(NT):
                    step(dve.max(m8[:, t, :], rt[:, 1, t, :]))
                sync()
                for t in range(NT):
                    step(dve.max_index(ix[:, t, :], m8[:, t, :], rt[:, 1, t, :]))
                sync()

            def one_hot(k):
                step(dve.tensor_copy(rk[:, 2, k], ix[:, :, k]))
                sync()
                step(dve.tensor_tensor(rt[:, 2 + k], iota8[:, :].unsqueeze(1).to_broadcast([P, NT, NX]), over_experts(rk[:, 2, k]), ALU.is_equal))

            def places(k, rank, cap, low):
                w_, e_ = rk[:, 1, k], rk[:, 2, k]
                step(dve.tensor_scalar(rk[:, 5, k], rank, float(cap), None, ALU.is_lt))
                step(dve.scalar_tensor_tensor(rk[:, 6, k], e_, float(cap), rank, MULT, ADD))
                sync()
                step(dve.tensor_scalar(rk[:, 7, k], rk[:, 5, k], -1e6, 1e6, MULT, ADD))
                step(dve.tensor_tensor(idx[:, 1, k, :], rk[:, 6, k], rk[:, 5, k], MULT))
                step(dve.tensor_tensor(rk[:, 8, k], w_, rk[:, 5, k], MULT))
                sync()
                return step(dve.tensor_tensor(idx[:, 0, k, :], rk[:, 6, k], rk[:, 7, k], ADD))

            dve.wait_ge(s_x1, 16)
            layernorm(1, LN, D)
            router_probs(0)
            for k in range(2):
                one_hot(k)
            step(dve.tensor_tensor(rk[:, 3, 0], m8[:, :, 0], m8[:, :, 1], ADD))
            sync()
            step(dve.tensor_scalar(rk[:, 3, 0], rk[:, 3, 0], 1e-9, None, MAX))
            sync()
            step(dve.reciprocal(rk[:, 3, 1], rk[:, 3, 0]))
            sync()
            for k in range(2):
                step(dve.tensor_tensor(rk[:, 1, k], m8[:, :, k], rk[:, 3, 1], MULT))
            sync()
            for k in range(2):
                step(dve.tensor_tensor(rt[:, 5 + k], rt[:, 2 + k], over_experts(rk[:, 1, k]), MULT))
            sync()
            step(dve.tensor_tensor(rt[:, 7], rt[:, 2], rt[:, 3], ADD))
            step(dve.tensor_tensor(rt[:, 8], rt[:, 5], rt[:, 6], ADD))
            sync()
            step(dve.tensor_scalar(rt[:, 9], rt[:, 7], -1.0, None, ADD))
            sync()
            dve.tensor_tensor(rt[:, 4], rt[:, 8], rt[:, 9], ADD).then_inc(s_rt_in, 1)
            for j in range(6):
                m, hf = j // 2, j % 2
                dve.wait_ge(s_ssilu, j + 1)
                dve.tensor_tensor(SA[:, m, hf * NH:(hf + 1) * NH], SG[:, j % 2, :], bank(5 + 2 * (j % 2)), MULT).then_inc(s_sact, 1)
            dve.wait_ge(s_tri, 1)
            for n in range(2 * NT):
                t, k = n // 2, n % 2
                dve.wait_ge(s_rr_mm, n + 1)
                r_ = psum[:, 2 * (n % 2):2 * (n % 2) + 2, :].rearrange("p a b -> p (a b)")
                sync()
                step(dve.tensor_scalar(rjunk, r_, rk[:, 1, k, t:t + 1], 0.0, ALU.is_gt, ADD, accum_out=rk[:, 4, k, t:t + 1]))
                sync()
                if n:
                    dve.wait_ge(s_rank, n)
                dve.scalar_tensor_tensor(rjunk, r_, rk[:, 1, k, t:t + 1], earlier[:, N - P - t * P:2 * N - P - t * P], ALU.is_equal, MULT,
                                         accum_out=rk[:, 9, k, t:t + 1]).then_inc(s_rank, 1)
                dve.wait_ge(s_rank, n + 1)
                t, hf = n // 2, n % 2
                x_ = XN[:, t, hf * HD:(hf + 1) * HD]
                dve.wait_ge(s_so_mm, n + 1)
                dve.tensor_tensor(x_, bank(4 + n % 4, HD), x_, ADD).then_inc(s_so_ev, 1)
            for k in range(2):
                step(dve.tensor_tensor(rk[:, 10, k], rk[:, 4, k], rk[:, 9, k], ADD))
                sync()
                last = places(k, rk[:, 10, k], CAP0, 0)
            sync()
            step(dve.tensor_copy(rk[:, 11, 0], rk[:, 10, 0]))
            sync()
            dve.tensor_copy(rk[:, 11, 1], rk[:, 10, 0]).then_inc(s_idx, 1)

            def expert(e):
                for m in range(KM):
                    dve.wait_ge(s_silu, e * 3 + (m + 1))
                    dve.tensor_tensor(EA[:, m, :], EG[:, m % 2, :], bank(3 + 2 * (m % 2), CAP0), MULT).then_inc(s_act, 1)
            expert(0)
            with dve.Fori(1, NX) as e:
                expert(e)
            s_ga = (s_ga0, s_ga1, s_ga2, s_ga3)

            def combine(n, k, t, base, gathered):
                dve.wait_ge(s_ga[n % 4], 16 * (gathered + n // 4 + 1))
                if n or base:
                    dve.wait_ge(s_comb, base + n)
                dve.scalar_tensor_tensor(XN[:, t, :], GR[n % 4], rk[:, 8, k, t:t + 1], XN[:, t, :], MULT, ADD).then_inc(s_comb, 1)
            dve.wait_ge(s_so_ev, 16)
            for n in range(2 * NT):
                combine(n, n % 2, n // 2, 0, 0)
            dve.wait_ge(s_comb, 2 * NT)

            h_ = cut(HN, [NT, RIN[0]])
            dve.wait_ge(s_emb, 32)
            step(dve.tensor_copy(ntypef[:, :], ntype[:, :]))
            layernorm(2, h_, RIN[0])
            for j in range(R):
                step(dve.tensor_scalar(mx[:, j, :], ntypef[:, :], float(j), None, ALU.is_equal))
            sync()
            for j in range(R):
                for t in range(NT):
                    e_ = h_[:, t, D:D + TD]
                    if j == 0:
                        step(dve.tensor_scalar(e_, emb[:, j, :], mx[:, j, t:t + 1], None, MULT))
                    else:
                        step(dve.scalar_tensor_tensor(e_, emb[:, j, :], mx[:, j, t:t + 1], e_, MULT, ADD))
                sync()
            dve.wait_ge(s_ln, 3 * NT)
            dve.tensor_copy(rd2[:, :], ntypef[:, :]).then_inc(s_hn, 1)
            y0 = 0
            for lay in range(3):
                ft, fo = RIN[lay] // P, ROUT[lay]
                fh = fo // 2
                a_ = cut(13312, [NT, fo])
                extra = 2 if lay == 0 else 0
                per = 2 * ft + extra
                dve.wait_ge(s_rb, 16 * (lay + 1))
                for g in range(16):
                    t, hf = g // 2, g % 2
                    dve.wait_ge(s_z_mm, 64 * lay + g + 1)
                    if lay:
                        dve.wait_ge(s_relu, 16 * lay)
                    dve.tensor_tensor(a_[:, t, hf * fh:(hf + 1) * fh], bank(4 + g % 4, fh), bias_bc[:, hf * fh:(hf + 1) * fh], ADD).then_inc(s_z_ev, 1)
                PERR = 4 if lay == 0 else 0
                with dve.Fori(0, R) as r:
                    if PERR:
                        ch.turn(r, 0, PERR)
                    yb = r * per + (y0 + 2 * ft)
                    if extra:
                        for hf in range(2):
                            o_ = inv.rearrange("p a b -> p (a b)")[:, bass.ds(r * N + hf * NH, NH)]
                            dve.wait_ge(s_y_mm, yb + hf + 1)
                            step(dve.tensor_scalar(rjunk2[:, 0, :], bank(hf), 1.0, None, MAX))
                            sync()
                            step(dve.reciprocal(rjunk2[:, 1, :], rjunk2[:, 0, :]))
                            sync()
                            dve.scalar_tensor_tensor(o_, bank(hf), 1.0, rjunk2[:, 1, :], MIN, MULT).then_inc(s_y_ev, 1)
                            dve.wait_ge(s_y_ev, yb + hf + 1)
                    for g in range(extra, per):
                        n = g - extra
                        f, hf = n // 2, g % 2
                        dve.wait_ge(s_y_mm, yb + g + 1)
                        dve.tensor_tensor(YT[:, f, hf * NH:(hf + 1) * NH], bank(g % 4), inv.rearrange("p a b -> p (a b)")[:, bass.ds(r * N + hf * NH, NH)], MULT).then_inc(s_y_ev, 1)
                    for g in range(16):
                        t, hf = g // 2, g % 2
                        o_ = a_[:, t, hf * fh:(hf + 1) * fh]
                        dve.wait_ge(s_z_mm, r * 16 + (64 * lay + 16 + g + 1))
                        dve.wait_ge(s_z_ev, r * 16 + (64 * lay + g + 1))
                        dve.tensor_tensor(o_, bank(4 + g % 4, fh), o_, ADD).then_inc(s_z_ev, 1)
                if PERR:
                    ch.leave(R, PERR)
                y0 += 2 * ft + R * per
            dve.wait_ge(s_z_ev, 3 * 64)
            for g in range(16):
                t, hf = g // 2, g % 2
                x_ = XN[:, t, hf * HD:(hf + 1) * HD]
                dve.scalar_tensor_tensor(x_, cut(13312, [NT, D])[:, t, hf * HD:(hf + 1) * HD], 0.0, x_, MAX, ADD).then_inc(s_x3, 1)

            dve.wait_ge(s_x3, 16)
            layernorm(3, LN, D)
            router_probs(1)
            one_hot(0)
            step(dve.tensor_copy(rk[:, 1, 0], m8[:, :, 0]))
            sync()
            dve.tensor_copy(rk[:, 3, 0], rk[:, 1, 0]).then_inc(s_rt_in, 1)
            dve.wait_ge(s_rr_mm, 2 * NT + 1)
            step(dve.tensor_tensor(rt[:, 5], psum[:, 0, 0:NT * NX].rearrange("p (a b) -> p a b", a=NT), rt[:, 2], MULT))
            sync()
            step(dve.tensor_reduce(rk[:, 4, 0], rt[:, 5], AX.X, ADD))
            sync()
            step(dve.tensor_scalar(rk[:, 10, 0], rk[:, 4, 0], 1.0, None, ADD))
            sync()
            places(0, rk[:, 10, 0], C1, 0)
            sync()
            dve.tensor_copy(rk[:, 11, 0], rk[:, 10, 0]).then_inc(s_idx, 1)
            s_fw = (s_fw0, s_fw1)

            def expert1(e, i, b, reuse):
                dve.wait_ge(s_fw[b], i * 64 + 64)
                for hf in range(2):
                    dve.wait_ge(s_f2_mm, e * 2 + (hf + 1))
                    if reuse and hf == 0:
                        dve.wait_ge((s_fs0, s_fs1)[b], i * 16)
                    dve.tensor_tensor(GO[:, b, hf * HD:(hf + 1) * HD], bank(6 + hf, HD), GB[b][:, hf * HD:(hf + 1) * HD], ADD).then_inc(s_f3, 1)
            expert1(0, 0, 0, False)
            expert1(1, 0, 1, False)
            with dve.Fori(1, NX // 2) as i:
                expert1(i * 2, i, 0, True)
                expert1(i * 2 + 1, i, 1, True)
            for n in range(NT):
                combine(n, 0, n, 2 * NT, 4)


_INS = ['x', 'src', 'dst', 'edge_type_3', 'node_type_3', 'L0_gnn_W1', 'L0_gnn_a_src1', 'L0_gnn_a_dst1', 'L0_gnn_b1', 'L0_gnn_W2', 'L0_gnn_a_src2', 'L0_gnn_a_dst2', 'L0_gnn_b2', 'L0_ffn_Wr', 'L0_ffn_w1', 'L0_ffn_w3', 'L0_ffn_w2', 'L0_ffn_s1', 'L0_ffn_s3', 'L0_ffn_s2', 'L1_gnn_node_emb', 'L1_gnn_w_rel1', 'L1_gnn_w_root1', 'L1_gnn_b1', 'L1_gnn_w_rel2', 'L1_gnn_w_root2', 'L1_gnn_b2', 'L1_gnn_w_rel3', 'L1_gnn_w_root3', 'L1_gnn_b3', 'L1_ffn_router_w', 'L1_ffn_w1', 'L1_ffn_b1', 'L1_ffn_w2', 'L1_ffn_b2']
_OUTS = [((1024, 768), 'float32')]
DBG = False


def kernel(**inputs):
    import numpy as _np
    import concourse.bacc as _bacc
    from concourse import mybir as _mybir
    from concourse.bass_utils import run_bass_kernel_spmd as _run

    nc = _bacc.Bacc("TRN2", target_bir_lowering=False, num_devices=1)
    arrays, aps = {}, {}
    for name in _INS:
        a = _np.ascontiguousarray(inputs[name])
        arrays[f"in_{name}_dram"] = a
        aps[name] = nc.dram_tensor(f"in_{name}_dram", a.shape, _mybir.dt.from_np(a.dtype), kind="ExternalInput").ap()
    shape, dtype = _OUTS[0]
    out = nc.dram_tensor("out_0_dram", shape, _mybir.dt.from_np(_np.dtype(dtype)), kind="ExternalOutput").ap()
    dbg = nc.dram_tensor("dbg", shape, _mybir.dt.float32, kind="ExternalOutput").ap() if DBG else None
    build(nc, aps, out, dbg)
    r = _run(nc, [arrays], core_ids=[0])
    return r.results[0]["out_0_dram"]
```

```python
import concourse.bass as bass
from concourse import mybir
from contextlib import ExitStack

fp32 = mybir.dt.float32
bf16 = mybir.dt.bfloat16
fp16 = mybir.dt.float16
fp32r = mybir.dt.float32r
i32 = mybir.dt.int32
u32 = mybir.dt.uint32
u16 = mybir.dt.uint16
ALU = mybir.AluOpType
ACT = mybir.ActivationFunctionType
AX = mybir.AxisListType
MULT, ADD, SUB, MAX, MIN = ALU.mult, ALU.add, ALU.subtract, ALU.max, ALU.min


class Chain:

    def __init__(self, eng, sem):
        self.eng, self.sem, self.base, self.k = eng, sem, 0, 0

    def step(self, ins):
        self.k += 1
        return ins.then_inc(self.sem, 1)

    def sync(self):
        self.eng.wait_ge(self.sem, self.base + self.k)

    def turn(self, i, first, per):
        if self.k or isinstance(self.base, int):
            self.before = self.base + self.k
        self.base, self.k = (i - first) * per + self.before, 0

    def leave(self, turns, per):
        assert self.k == per, (self.k, per)
        self.base, self.k = self.before + turns * per, 0


def build(nc, io, out):
    P = 128
    N, D = io['x'].shape
    E, = io['src'].shape
    NT = N // P
    KD = D // P
    R = 3
    NBK = R * NT
    EC = E // P
    NCH = EC + NBK
    H1 = io['L0_gnn_a_src1'].shape[0]
    HD = D // 2
    NH = N // 2
    NEG = -1e30
    EPS = 1e-5
    NX = io['L0_ffn_Wr'].shape[1]
    M0 = io['L0_ffn_s1'].shape[1]
    KM = M0 // P
    CAP0 = -(-N * 2 * 5 // (NX * 4))
    CB0 = [(b, min(P, CAP0 - b)) for b in range(0, CAP0, P)]
    C1 = N // NX
    TD = io['L1_gnn_node_emb'].shape[1]
    RG = [('L1_gnn_w_rel1', 'L1_gnn_w_root1', 'L1_gnn_b1'),
          ('L1_gnn_w_rel2', 'L1_gnn_w_root2', 'L1_gnn_b2'),
          ('L1_gnn_w_rel3', 'L1_gnn_w_root3', 'L1_gnn_b3')]
    RIN = [io[w].shape[0] for _, w, _ in RG]
    ROUT = [io[w].shape[1] for _, w, _ in RG]
    assert EC * P == E and CAP0 == 320 and NBK * P + E <= NCH * P

    ctx = ExitStack()
    with ctx:
        def sb(name, shape, dt=fp32):
            return ctx.enter_context(nc.sbuf_tensor(name, shape, dt))

        def sem(name):
            return ctx.enter_context(nc.semaphore(name))

        def scratch(name, shape, dt=fp32):
            return nc.dram_tensor(name, shape, dt, kind="Internal").ap()

        slots = scratch("slots", [P * NCH, 1], i32)
        adj_d = scratch("adj_d", [R, P, NT * N], u16)
        disp0_d = scratch("disp0_d", [NX * CAP0, D])
        eout0_d = scratch("eout0_d", [NX * CAP0, D])
        disp1_d = scratch("disp1_d", [NX * C1, D])
        eout1_d = scratch("eout1_d", [NX * C1, D])
        hs_d = scratch("hs_d", [H1, P, NT * D])

        WORDS = 51712
        base = -(-nc.sbuf_base // 32) * 32
        arena = sb("arena", [P, WORDS])

        def part(name, at, shape, dt=fp32r):
            n = 1
            for d in shape:
                n *= d
            assert at + n <= WORDS
            return nc.alloc_sbuf_tensor_at(name, [P] + shape, dt, offset=base + 4 * at)

        ones = sb("ones", [P, P])
        ident = sb("ident", [P, P])
        before = sb("before", [P, P])
        iota8 = sb("iota8", [P, 8])
        def cut(at, shape, dt=fp32):
            n = 1
            for s in shape:
                n *= s
            per = {fp32: 1, i32: 1, u32: 1, bf16: 2, fp16: 2, u16: 2}[dt]
            v = arena[:, at:at + n // per]
            assert at + n // per <= WORDS
            if dt != fp32:
                v = v.bitcast(dt)
            if len(shape) == 2:
                v = v.rearrange("p (a b) -> p a b", a=shape[0])
            if len(shape) == 3:
                v = v.rearrange("p (a b c) -> p a b c", a=shape[0], b=shape[1])
            return v

        XTh = part("XTh", 0, [KD, N])
        XTl = part("XTl", 6144, [KD, N])
        XL = cut(12288, [NT, D])
        HS = cut(12288, [NT, D])
        A_r = cut(18432, [NBK * N], u16)
        onehot = cut(18432, [NBK, EC])
        running = cut(21696, [NBK, EC])
        cmp = cut(24960, [NCH, NBK])
        iota = cut(28800, [N])
        zero = cut(29824, [D])
        W1r = part("W1r", 30720, [2, KD, HD], fp32)
        W1h = part("W1h", 35328, [2, KD, HD])
        W1l = part("W1l", 39936, [2, KD, HD])
        D1 = cut(44544, [2, N], bf16)
        S1 = cut(45568, [2, P], bf16)
        iotah = cut(45696, [N], fp16)
        recf = cut(46208, [2, NCH + 2])
        bk = cut(46532, [10, NBK + 1])
        bki = cut(46782, [NBK], i32)
        boff = cut(46806, [NCH])
        boffi = cut(46966, [NCH], i32)
        o = 47126
        edges = cut(o, [3, EC], i32)
        ework = cut(o + 408, [4, EC], i32)
        dots_junk = cut(o, [D])
        keyf = cut(o + 952, [EC])
        slotf = cut(o + 1088, [EC])
        code = cut(o + 1224, [EC], i32)
        sloti = cut(o + 1360, [3, EC], i32)
        row = cut(o + 1768, [EC], i32)
        empty = cut(o + 1904, [NCH], i32)
        recs = cut(o + 2064, [3, NCH], i32)
        a_bc = cut(49670, [2, D])
        MN = cut(30720, [NT, N], bf16)
        MK = cut(34816, [NT, N], bf16)
        junk = cut(47616, [N])
        H = cut(0, [NT, D])
        PM = cut(6144, [NT, N])
        OTh = part("OTh", 14336, [KD, N])
        OTl = part("OTl", 20480, [KD, N])
        W2h = part("W2h", 26624, [KD, D])
        W2l = part("W2l", 31232, [KD, D])
        W2r = part("W2r", 35840, [2, D], fp32)
        ACC = cut(37376, [NT, D])
        AT = cut(43520, [NT, N], u16)
        ET = cut(47616, [2, NH])
        Y = part("Y", 48640, [2, NH], fp32)
        RD = cut(49664, [NH])
        PS = cut(50176, [NH])
        DG = cut(50688, [N])
        MN2 = cut(0, [NT, N], bf16)
        MK2 = cut(6144, [NT, N], bf16)
        junk2 = cut(10240, [N])
        a2_bc = cut(11264, [2, D])
        XN = cut(0, [NT, D])
        b2_bc = cut(26624, [D])

        LN = cut(6144, [NT, D])
        LT = cut(12288, [KD, N])
        EW = [(cut(18432 + 6912 * b, [KD, M0]), cut(20736 + 6912 * b, [KD, M0]), cut(23040 + 6912 * b, [KM, D])) for b in range(2)]
        SA = cut(25344, [KM, N])
        SG = cut(28416, [2, NH])
        SW = (cut(32256, [KD, M0]), cut(34560, [KD, M0]), cut(36864, [KM, D]))
        DR = [cut(39168 + 2304 * b, [len(CB0), D]) for b in range(2)]
        DT = cut(43776, [KD, CAP0])
        EA = cut(45696, [KM, CAP0])
        EG = cut(46656, [2, CAP0])
        EO = cut(47296, [len(CB0), D])
        rowsT = cut(43776, [3, N])
        rjunk = cut(46848, [N])
        earlier = cut(49600, [2 * N - P], bf16)
        rt = cut(50560, [10, NT, NX])
        Wr = cut(51328, [KD, NX])
        rk = cut(51504, [12, 2, NT])
        m8 = cut(51200, [NT, 8])
        ix = cut(51264, [NT, 8], u32)
        GR = [cut(6144 + D * b, [D]) for b in range(4)]
        FT0 = RIN[0] // P
        YTh = part("YTh", 6144, [FT0, NH])
        YTl = part("YTl", 9728, [FT0, NH])
        RA = 13312
        AF = cut(20480, [NT, NH])
        AR = cut(24576, [NT, N], u16)
        RWh = part("RWh", 28672, [FT0, ROUT[0]])
        RWl = part("RWl", 34944, [FT0, ROUT[0]])
        RWr = part("RWr", 41216, [2, ROUT[0]], fp32)
        HN = 43008
        emb = cut(50176, [R, TD])
        csum = cut(50176, [NH])
        bias_bc = cut(50688, [ROUT[0]])
        inv = cut(51584, [R * NT])
        inv_r = cut(51608, [NT])
        cwork = cut(51616, [2, NT // 2])
        GW = [(cut(18432 + 4608 * b, [KD, M0]), cut(20736 + 4608 * b, [KM, D])) for b in range(2)]
        GB = [cut(27648 + D * b, [D]) for b in range(2)]
        GD = [cut(29184 + D * b, [D]) for b in range(2)]
        GT = cut(30720, [KD, C1])
        GA = cut(31488, [KM, C1])
        GO = cut(31872, [2, D])
        gb1 = [cut(33408 + 4 * b, [KM]) for b in range(2)]

        idx = sb("idx", [P, 2, 2, NT], i32)
        ntype = sb("ntype", [P, NT], i32)
        ntypef = sb("ntypef", [P, NT])
        identb = sb("identb", [P, P], bf16)
        alpha = sb("alpha", [P, 2, NT])
        VA = sb("VA", [P, (H1 + 1) * 4 * NT])
        cur = sb("cur", [P, 2, NT])
        mx = sb("mx", [P, 4, NT])
        b1c = sb("b1c", [P, KD])
        stats = sb("stats", [P, NT, 2, 6])
        mv = sb("mv", [P, NT, 2])
        rstd = sb("rstd", [P, NT])
        rd2 = sb("rd2", [P, NT])

        psum = ctx.enter_context(nc.psum_tensor("psum", [P, 8, 512], fp32))

        s_edges = sem("s_edges")
        s_const = sem("s_const")
        dch = sem("dch")
        ach = sem("ach")
        s_cnt = sem("s_cnt")
        s_tot = sem("s_tot")
        s_empty = sem("s_empty")
        s_pre = sem("s_pre")
        s_row = sem("s_row")
        s_scat = sem("s_scat")
        s_recs = sem("s_recs")
        s_hot = sem("s_hot")
        s_pair = sem("s_pair")
        s_added = sem("s_added")
        s_x = sem("s_x")
        s_zero = sem("s_zero")
        s_var = sem("s_var")
        s_std = sem("s_std")
        s_ln = sem("s_ln")
        s_xt_mm = sem("s_xt_mm")
        s_xt_ev = sem("s_xt_ev")
        s_spill = sem("s_spill")
        s_mn = sem("s_mn")
        s_mk_mm = sem("s_mk_mm")
        s_mk_ev = sem("s_mk_ev")
        s_xt_hi = sem("s_xt_hi")
        s_w1a = sem("s_w1a")
        s_w1b = sem("s_w1b")
        s_w1h = sem("s_w1h")
        s_w1l = sem("s_w1l")
        s_hs = [sem(f"s_hs{t}") for t in range(NT)]
        s_dot = sem("s_dot")
        s_a = sem("s_a")
        s_b1 = sem("s_b1")
        s_h_mm = sem("s_h_mm")
        s_h_ev = sem("s_h_ev")
        s_hl = sem("s_hl")
        s_w2r = [sem(f"s_w2r{n}") for n in range(2)]
        s_w2h = sem("s_w2h")
        s_w2l = sem("s_w2l")
        s_diag = sem("s_diag")
        s_bc = sem("s_bc")
        s_mx = sem("s_mx")
        s_exp = sem("s_exp")
        s_larger = sem("s_larger")
        s_P = sem("s_P")
        s_ps = sem("s_ps")
        s_den = sem("s_den")
        s_rd = sem("s_rd")
        s_p_mm = sem("s_p_mm")
        s_acc_ev = sem("s_acc_ev")
        s_agg_mm = sem("s_agg_mm")
        s_y = sem("s_y")
        s_elu = sem("s_elu")
        s_efix = sem("s_efix")
        s_zs = sem("s_zs")
        s_oh = sem("s_oh")
        s_ot = sem("s_ot")
        s_m2 = sem("s_m2")
        s_m2_mm = sem("s_m2_mm")
        s_m2_ev = sem("s_m2_ev")
        s_at2 = sem("s_at2")
        pch = sem("pch")
        s_xr = sem("s_xr")
        s_g2_mm = sem("s_g2_mm")
        s_x1 = sem("s_x1")
        s_wr = sem("s_wr")
        s_sw = sem("s_sw")
        s_tri = sem("s_tri")
        s_lg = sem("s_lg")
        s_ct = sem("s_ct")
        s_exps = sem("s_exps")
        s_rt_in = sem("s_rt_in")
        s_rt_mm = sem("s_rt_mm")
        s_rt_ev = sem("s_rt_ev")
        s_rr_mm = sem("s_rr_mm")
        s_rank = sem("s_rank")
        s_idx = sem("s_idx")
        s_disp = sem("s_disp")
        s_sg_mm = sem("s_sg_mm")
        s_ssilu = sem("s_ssilu")
        s_sact = sem("s_sact")
        s_so_mm = sem("s_so_mm")
        s_so_ev = sem("s_so_ev")
        s_ew0 = sem("s_ew0")
        s_ew1 = sem("s_ew1")
        s_dr0 = sem("s_dr0")
        s_dr1 = sem("s_dr1")
        s_dt_mm = sem("s_dt_mm")
        s_dt_ev = sem("s_dt_ev")
        s_gu_mm = sem("s_gu_mm")
        s_silu = sem("s_silu")
        s_act = sem("s_act")
        s_eo_mm = sem("s_eo_mm")
        s_eo_ev = sem("s_eo_ev")
        s_es = sem("s_es")
        s_ga0 = sem("s_ga0")
        s_ga1 = sem("s_ga1")
        s_ga2 = sem("s_ga2")
        s_ga3 = sem("s_ga3")
        s_comb = sem("s_comb")
        s_emb = sem("s_emb")
        s_hn = sem("s_hn")
        s_y_mm = sem("s_y_mm")
        s_y_ev = sem("s_y_ev")
        s_z_mm = sem("s_z_mm")
        s_z_ev = sem("s_z_ev")
        s_rw = [sem(f"s_rw{n}") for n in range(2)]
        s_rwh = sem("s_rwh")
        s_rwl = sem("s_rwl")
        s_yh = sem("s_yh")
        s_cs = sem("s_cs")
        s_cm = sem("s_cm")
        s_cv = sem("s_cv")
        s_ar = sem("s_ar")
        s_af = sem("s_af")
        s_rb = sem("s_rb")
        s_relu = sem("s_relu")
        s_x3 = sem("s_x3")
        s_ft_mm = sem("s_ft_mm")
        s_ft_ev = sem("s_ft_ev")
        s_f1_mm = sem("s_f1_mm")
        s_f1 = sem("s_f1")
        s_f2_mm = sem("s_f2_mm")
        s_f2 = sem("s_f2")
        s_f3 = sem("s_f3")
        s_fs0 = sem("s_fs0")
        s_fs1 = sem("s_fs1")
        s_fw0 = sem("s_fw0")
        s_fw1 = sem("s_fw1")
        s_fr0 = sem("s_fr0")
        s_fr1 = sem("s_fr1")
        s_disp1 = sem("s_disp1")
        s_out = sem("s_out")

        LOWS = (20, 42, 64, 86)

        block = ctx.enter_context(nc.Block())
        w1_v = io['L0_gnn_W1'].rearrange("(k p) (u c) -> u p k c", p=P, u=2 * H1)
        w2_v = io['L0_gnn_W2'].rearrange("(v p) c -> v p c", p=P)
        b1_v = io['L0_gnn_b1'].rearrange("(h m p) -> h p m", p=P, h=H1)

        def bank(b, n=512):
            return psum[:, b, 0:n]

        @block.sync
        def _(sp):
            for n, a in enumerate((io['src'], io['dst'], io['edge_type_3'])):
                sp.dma_start(edges[:, n, :], a.rearrange("(p c) -> p c", p=P)).then_inc(s_edges, 16)
            sp.dma_start(XL, io['x'].rearrange("(t p) d -> p t d", p=P)).then_inc(s_x, 16)
            sp.wait_ge(s_empty, 1)
            sp.dma_start(slots.rearrange("(p c) o -> p (c o)", p=P), empty).then_inc(s_pre, 16)
            def load_a(i):
                for k, name in enumerate(('L0_gnn_a_src1', 'L0_gnn_a_dst1')):
                    sp.dma_start(a_bc[:, k, :], io[name][bass.ds(i, 1), :].rearrange("o d -> (o d)").partition_broadcast(P)).then_inc(s_a, 16)

            def load_w1(i, hf):
                sp.dma_start(W1r[:, hf], w1_v[bass.ds(i * 2 + hf, 1)].rearrange("o p k c -> (o p) k c")).then_inc((s_w1a, s_w1b)[hf], 16)
            load_w1(0, 0)
            load_w1(0, 1)
            load_a(0)
            sp.wait_ge(s_empty, 2)
            for buf in (disp0_d, disp1_d):
                rows = buf.rearrange("(n p) d -> n p d", p=P)
                for n in range(rows.shape[0]):
                    sp.dma_start(rows[n], zero).then_inc(s_zero, 16)
            sp.dma_start(b1c[:, :], b1_v[0], allow_slow_non_contiguous=True).then_inc(s_b1, 16)

            def feature_loads(i):
                for hf in range(2):
                    sp.wait_ge(s_w1l, i * 2 + (hf - 1))
                    load_w1(i, hf)
                sp.wait_ge(s_dot, i * NT)
                load_a(i)
            feature_loads(1)
            feature_loads(2)
            sp.wait_ge(s_scat, 16 * EC)
            sp.dma_start(recs[:, 0, :], slots.rearrange("(p c) o -> p (c o)", p=P)).then_inc(s_recs, 16)
            with sp.Fori(3, H1) as i:
                feature_loads(i)
            sp.wait_ge(s_added, NCH + 2)
            for r in range(R):
                sp.dma_start(adj_d[r], A_r[:, r * NT * N:(r + 1) * NT * N]).then_inc(s_spill, 16)

            def load_h(i):
                sp.dma_start(H.rearrange("p t d -> p (t d)"), hs_d[bass.ds(i, 1)].rearrange("o p n -> (o p) n")).then_inc(s_hl, 16)
            sp.wait_ge(s_h_mm, H1 * 16)
            for t in range(NT):
                sp.wait_ge(s_hs[t], H1 * 16)
            load_h(0)
            sp.wait_ge(s_mx, H1)

            def head_loads(i, first=False, last=False):
                for k in range(KD):
                    if k >= 2 or not first:
                        sp.wait_ge(s_w2l, i * KD + (k - 1))
                    sp.dma_start(W2r[:, k % 2, :], w2_v[bass.ds(i * KD + k, 1)].rearrange("o p c -> (o p) c")).then_inc(s_w2r[k % 2], 16)
                if not last:
                    sp.wait_ge(s_agg_mm, (i + 1) * 12)
                    load_h(i + 1)
                    sp.wait_ge(s_elu, (i + 1) * 12)
                    sp.dma_start(b1c[:, :], b1_v[bass.ds(i + 1, 1)].rearrange("o p m -> (o p) m"), allow_slow_non_contiguous=True).then_inc(s_b1, 16)
            head_loads(0, first=True)
            with sp.Fori(1, H1 - 1) as i:
                head_loads(i)
            head_loads(H1 - 1, last=True)
            sp.wait_ge(s_agg_mm, H1 * 12)
            sp.wait_ge(s_ps, H1 * 2)
            for k, name in enumerate(('L0_gnn_a_src2', 'L0_gnn_a_dst2')):
                sp.dma_start(a2_bc[:, k, :], io[name].rearrange("o d -> (o d)").partition_broadcast(P)).then_inc(s_a, 16)
            sp.wait_ge(s_m2_mm, NT)
            sp.dma_start(XN, io['x'].rearrange("(t p) d -> p t d", p=P)).then_inc(s_xr, 16)
            sp.wait_ge(s_p_mm, H1 * 16)
            sp.dma_start(b2_bc, io['L0_gnn_b2'].partition_broadcast(P)).then_inc(s_xr, 16)

            sp.wait_ge(s_x1, 16)
            sp.dma_start(Wr, io['L0_ffn_Wr'].rearrange("(k p) e -> p k e", p=P)).then_inc(s_wr, 16)
            for w, name in zip(SW, ('L0_ffn_s1', 'L0_ffn_s3', 'L0_ffn_s2')):
                sp.dma_start(w, io[name].rearrange("(k p) n -> p k n", p=P)).then_inc(s_sw, 16)
            ew_v = [io[name].rearrange("e (k p) n -> e p k n", p=P) for name in ('L0_ffn_w1', 'L0_ffn_w3', 'L0_ffn_w2')]
            s_ew, s_dr = (s_ew0, s_ew1), (s_dr0, s_dr1)

            def expert_loads(e, b, reuse):
                if reuse:
                    sp.wait_ge(s_eo_mm, (e - 1) * 6)
                for w, v in zip(EW[b], ew_v):
                    sp.dma_start(w, v[bass.ds(e, 1)].rearrange("o p k n -> (o p) k n")).then_inc(s_ew[b], 16)
                if not reuse:
                    sp.wait_ge(s_disp, 16 * 2 * NT)
                for j, (c0, cn) in enumerate(CB0):
                    sp.dma_start(DR[b][0:cn, j, :], disp0_d[bass.ds(e * CAP0 + c0, cn), :]).then_inc(s_dr[b], 16)

            expert_loads(0, 0, False)
            sp.wait_ge(s_so_mm, 16)
            expert_loads(1, 1, False)
            with sp.Fori(1, NX // 2) as i:
                expert_loads(i * 2, 0, True)
                expert_loads(i * 2 + 1, 1, True)

            sp.dma_start(ntype[:, :], io['node_type_3'].rearrange("(t p) -> p t", p=P), allow_slow_non_contiguous=True).then_inc(s_emb, 16)
            sp.wait_ge(s_eo_ev, 6 * NX)
            sp.wait_ge(s_es, 48 * NX)
            sp.dma_start(emb.rearrange("p a b -> p (a b)"), io['L1_gnn_node_emb'].rearrange("a b -> (a b)").partition_broadcast(P)).then_inc(s_emb, 16)
            for lay in range(3):
                ft, fo = RIN[lay] // P, ROUT[lay]
                rel, root, bias = (io[n] for n in RG[lay])
                kb = sum(RIN[:lay]) // P * 4

                def weight_loads(w, rows, row0, first=False):
                    for k in range(ft):
                        if k >= 2 or not first:
                            sp.wait_ge(s_rwl, w * ft + (kb + max(k - 1, 0)))
                        sp.dma_start(RWr[:, k % 2, 0:fo], rows[bass.ds(row0 + k, 1)].rearrange("o p n -> (o p) n")).then_inc(s_rw[k % 2], 16)
                weight_loads(0, root.rearrange("(k p) n -> k p n", p=P), 0, first=lay == 0)
                sp.wait_ge(s_z_ev, lay * 64 - 48) if lay else sp.wait_ge(s_hn, 1)
                sp.dma_start(bias_bc[:, 0:fo], bias.partition_broadcast(P)).then_inc(s_rb, 16)
                rel_v = rel.rearrange("r (k p) n -> (r k) p n", p=P)

                def relation_loads(r, first=False):
                    if not first:
                        sp.wait_ge(s_af, r * 2 + lay * R * 2)
                    sp.dma_start(AR.rearrange("p a b -> p (a b)"), adj_d[bass.ds(r, 1)].rearrange("o p n -> (o p) n")).then_inc(s_ar, 16)
                    weight_loads(r + 1, rel_v, r * ft)
                relation_loads(0, first=lay == 0)
                with sp.Fori(1, R) as r:
                    relation_loads(r)

            sp.wait_ge(s_x3, 16)
            sp.dma_start(Wr, io['L1_ffn_router_w'].rearrange("(k p) e -> p k e", p=P)).then_inc(s_wr, 16)
            fw_v = [io[name].rearrange("e (k p) n -> e p k n", p=P) for name in ('L1_ffn_w1', 'L1_ffn_w2')]
            fb_v = io['L1_ffn_b1'].rearrange("e (m p) -> e p m", p=P)
            s_fw, s_fr = (s_fw0, s_fw1), (s_fr0, s_fr1)

            def expert1_loads(e, b, reuse):
                if reuse:
                    sp.wait_ge(s_f2, (e - 1) * 2)
                for w, v in zip(GW[b], fw_v):
                    sp.dma_start(w, v[bass.ds(e, 1)].rearrange("o p k n -> (o p) k n")).then_inc(s_fw[b], 16)
                sp.dma_start(gb1[b], fb_v[bass.ds(e, 1)].rearrange("o p m -> (o p) m"), allow_slow_non_contiguous=True).then_inc(s_fw[b], 16)
                sp.dma_start(GB[b], io['L1_ffn_b2'][bass.ds(e, 1), :].rearrange("o d -> (o d)").partition_broadcast(P)).then_inc(s_fw[b], 16)
                if not reuse:
                    sp.wait_ge(s_disp1, 16 * NT)
                sp.dma_start(GD[b], disp1_d[bass.ds(e * C1, C1), :]).then_inc(s_fr[b], 16)

            expert1_loads(0, 0, False)
            expert1_loads(1, 1, False)
            with sp.Fori(1, NX // 2) as i:
                expert1_loads(i * 2, 0, True)
                expert1_loads(i * 2 + 1, 1, True)
            sp.wait_ge(s_comb, 2 * NT + NT)
            sp.dma_start(out.rearrange("(t p) d -> p t d", p=P), XN).then_inc(s_out, 16)
            sp.wait_ge(s_out, 16)

        @block.gpsimd
        def _(pool):
            pool.memset(empty, -1).then_inc(s_empty, 1)
            pool.memset(zero, 0.0).then_inc(s_empty, 1)
            pool.memset(ones[:, :], 1.0).then_inc(s_const, 1)
            pool.iota(iota, [[1, N]], base=0, channel_multiplier=0, allow_small_or_imprecise_dtypes=True).then_inc(s_const, 1)
            pool.iota(iota8[:, :], [[1, 8]], base=0, channel_multiplier=0, allow_small_or_imprecise_dtypes=True).then_inc(s_const, 1)
            pool.wait_ge(s_const, 3)
            pool.affine_select(out=before[:, :], in_=ones[:, :], compare_op=ALU.is_gt, fill=0.0,
                               base=0, pattern=[[1, P]], channel_multiplier=-1).then_inc(s_const, 1)
            pool.affine_select(out=ident[:, :], in_=ones[:, :], compare_op=ALU.is_equal, fill=0.0,
                               base=0, pattern=[[1, P]], channel_multiplier=-1).then_inc(s_const, 1)

            def low_half(i, hf):
                pool.wait_ge(s_w1h, i * 2 + (hf + 1))
                pool.tensor_tensor(W1l[:, hf], W1r[:, hf], W1h[:, hf].bitcast(fp32), SUB).then_inc(s_w1l, 1)
            low_half(0, 0)
            low_half(0, 1)
            pool.wait_ge(s_row, 1)
            pool.wait_ge(s_pre, 16)
            for c in range(EC):
                pool.indirect_dma_start(slots, bass.IndirectOffsetOnAxis(ap=row[:, c:c + 1], axis=0),
                                        code[:, c:c + 1], None).then_inc(s_scat, 16)
                if c in LOWS:
                    n = 2 + LOWS.index(c)
                    low_half(n // 2, n % 2)
            with pool.Fori(3, H1) as i:
                for hf in range(2):
                    low_half(i, hf)
            pc = Chain(pool, pch)

            def head(i, first=False):
                for hf in range(2):
                    d = slice(hf * NH, (hf + 1) * NH)
                    pool.wait_ge(s_P, i * 2 + (hf + 1))
                    if hf or not first:
                        pool.wait_ge(s_den, i * 2 + hf)
                    ins = pc.step(pool.tensor_tensor(PS, PM[:, 0, d], PM[:, 1, d], ADD))
                    for s in range(2, NT):
                        pc.sync()
                        ins = pool.tensor_tensor(PS, PS, PM[:, s, d], ADD)
                        if s < NT - 1:
                            pc.step(ins)
                    ins.then_inc(s_ps, 1)

                def low(n):
                    hf, f = n // KD, n % KD
                    d = slice(hf * NH, (hf + 1) * NH)
                    pool.wait_ge(s_oh, i * 12 + (n + 1))
                    pool.tensor_tensor(OTl[:, f, d], Y[:, n % 2, :], OTh[:, f, d].bitcast(fp32), SUB).then_inc(s_ot, 1)
                for n in range(2 * KD):
                    pool.wait_ge(s_efix, i * 12 + (n + 1))
                    pool.tensor_tensor(Y[:, n % 2, :], Y[:, n % 2, :], ET[:, n % 2, :], ADD).then_inc(s_zs, 1)
                    low(n)
                    if n < KD:
                        k = n
                        pool.wait_ge(s_w2h, i * KD + (k + 1))
                        pool.tensor_tensor(W2l[:, k, :], W2r[:, k % 2, :], W2h[:, k, :].bitcast(fp32), SUB).then_inc(s_w2l, 1)
            head(0, True)
            with pool.Fori(1, H1) as i:
                pc.turn(i, 1, 12)
                head(i)
            pc.leave(H1 - 1, 12)

            pool.wait_ge(s_P, H1 * 2 + 2)
            pool.affine_select(out=earlier, in_=ones[:, 0:1].to_broadcast([P, 2 * N - P]), compare_op=ALU.is_gt, fill=0.0,
                               base=N - P, pattern=[[-1, 2 * N - P]], channel_multiplier=1).then_inc(s_tri, 1)
            s_ga = (s_ga0, s_ga1, s_ga2, s_ga3)

            def scatter(k, t, rows, s):
                pool.indirect_dma_start(rows, bass.IndirectOffsetOnAxis(ap=idx[:, 0, k, t:t + 1], axis=0), LN[:, t, :], None,
                                        bounds_check=rows.shape[0] - 1, oob_is_err=False).then_inc(s, 16)

            def gather(n, k, t, rows, base):
                if n >= 4:
                    pool.wait_ge(s_comb, base + n - 3)
                pool.indirect_dma_start(GR[n % 4], None, rows, bass.IndirectOffsetOnAxis(ap=idx[:, 1, k, t:t + 1], axis=0)).then_inc(s_ga[n % 4], 16)

            pool.wait_ge(s_idx, 1)
            for t in range(NT):
                for k in range(2):
                    scatter(k, t, disp0_d, s_disp)
            pool.wait_ge(s_es, 48 * NX)
            for n in range(2 * NT):
                gather(n, n % 2, n // 2, eout0_d, 0)
            kb = 0
            for lay in range(3):
                ft, fo = RIN[lay] // P, ROUT[lay]

                def weights(w):
                    for k in range(ft):
                        pool.wait_ge(s_rwh, w * ft + (kb + k + 1))
                        pool.tensor_tensor(RWl[:, k, 0:fo], RWr[:, k % 2, 0:fo], RWh[:, k, 0:fo].bitcast(fp32), SUB).then_inc(s_rwl, 1)

                def sums(r, half):
                    pool.wait_ge(s_af, r * 2 + (half + 1))
                    if half or not isinstance(r, int):
                        pool.wait_ge(s_cm, r * 2 + half)
                    ins = pc.step(pool.tensor_tensor(csum, AF[:, 0, :], AF[:, 1, :], ADD))
                    for s in range(2, NT):
                        pc.sync()
                        ins = pool.tensor_tensor(csum, csum, AF[:, s, :], ADD)
                        if s < NT - 1:
                            pc.step(ins)
                    ins.then_inc(s_cs, 1)

                def relation(r):
                    sums(r, 0)
                    weights(r + 1)
                    sums(r, 1)
                weights(0)
                if lay == 0:
                    relation(0)
                    with pool.Fori(1, R) as r:
                        pc.turn(r, 1, 12)
                        relation(r)
                    pc.leave(R - 1, 12)
                else:
                    with pool.Fori(1, 1 + R) as w:
                        weights(w)
                kb += 4 * ft
            pool.wait_ge(s_idx, 2)
            for t in range(NT):
                scatter(0, t, disp1_d, s_disp1)
            for stored in (s_fs0, s_fs1):
                pool.wait_ge(stored, 16 * NX // 2)
            for n in range(NT):
                gather(n, 0, n, eout1_d, 2 * NT)

        @block.tensor
        def _(pe):
            def group(o_, pairs, s):
                for j, (l, r) in enumerate(pairs):
                    mm = pe.matmul(o_, l, r, start=(j == 0), stop=(j == len(pairs) - 1))
                mm.then_inc(s, 1)

            pe.wait_ge(s_const, 5)
            pe.wait_ge(s_cnt, 1)
            group(bank(0, NBK), [(before[:, :], bk[:, 2, 0:NBK])], s_tot)
            group(bank(1, NBK), [(ones[:, :], bk[:, 2, 0:NBK])], s_tot)
            pe.wait_ge(s_ln, NT)
            for g in range(2 * KD):
                k, hf = g // 2, g % 2
                if g >= 4:
                    pe.wait_ge(s_xt_ev, g - 3)
                for t in range(4):
                    mm = pe.transpose(psum[:, 4 + g % 4, t * P:(t + 1) * P], XL[:, 4 * hf + t, k * P:(k + 1) * P], ident[:, :])
                mm.then_inc(s_xt_mm, 1)

            def products(o_, pairs, s):
                n = 3 * len(pairs)
                j = 0
                for lh, ll, rh, rl in pairs:
                    for l, r in ((lh, rh), (lh, rl), (ll, rh)):
                        mm = pe.matmul(o_, l, r, start=(j == 0), stop=(j == n - 1))
                        j += 1
                mm.then_inc(s, 1)

            def h_group(i, g, first=False):
                hf, t = g // NT, g % NT
                if t == 0:
                    pe.wait_ge(s_w1l, i * 2 + (hf + 1))
                if g >= 4 or not first:
                    pe.wait_ge(s_h_ev, i * 16 + (g - 3))
                ts = slice(t * P, (t + 1) * P)
                products(bank(4 + g % 4, HD), [(XTh[:, k, ts], XTl[:, k, ts], W1h[:, hf, k, :], W1l[:, hf, k, :]) for k in range(KD)], s_h_mm)

            pe.wait_ge(s_xt_ev, 12)
            for i in range(3):
                for g in range(16):
                    h_group(i, g, i == 0)

            def pair(c, par):
                pe.wait_ge(s_hot, c + 1)
                pe.wait_ge(s_added, c + 1)
                for h in range(2):
                    mm = pe.matmul(bank(2 * par + h), S1[:, par, :], D1[:, par, 512 * h:512 * h + 512], start=True, stop=True)
                mm.then_inc(s_pair, 1)
            with pe.Fori(0, H1 - 3) as i:
                for j in range(16):
                    for par in range(2):
                        pair(i * 32 + (2 * j + par), par)
                    h_group(i + 3, j)
            pe.wait_ge(s_mn, 1)
            pe.wait_ge(s_added, NCH + 2)
            for j in range(NT):
                if j >= 4:
                    pe.wait_ge(s_mk_ev, j - 3)
                for t in range(NT):
                    mm = pe.transpose(psum[:, j % 4, :].bitcast(bf16)[:, t * P:(t + 1) * P], MN[:, t, j * P:(j + 1) * P], identb[:, :])
                mm.then_inc(s_mk_mm, 1)
            pe.wait_ge(s_mk_ev, NT)
            pe.wait_ge(s_h_ev, H1 * 16)

            def row_bc(count, b):
                pe.wait_ge(s_diag, count)
                for hf in range(2):
                    mm = pe.matmul(bank(b + hf), ones[:, :], DG[:, hf * 512:(hf + 1) * 512], start=True, stop=True)
                mm.then_inc(s_bc, 1)

            row_bc(1, 0)
            row_bc(2, 2)
            with pe.Fori(1, H1 // 2) as i:
                for b in range(2):
                    pe.wait_ge(s_mx, i * 2 + (b - 1))
                    row_bc(i * 2 + (b + 1), 2 * b)
            pe.wait_ge(s_mx, H1)
            row_bc(H1 + 1, 0)
            row_bc(H1 + 2, 2)

            def proj_groups(i):
                pe.wait_ge(s_w2l, i * KD + KD)
                pe.wait_ge(s_ot, i * 12 + 6)
                for g in range(16):
                    hf, t = g // NT, g % NT
                    if g < 3:
                        pe.wait_ge(s_y, i * 12 + (10 + g))
                    if g == 3:
                        pe.wait_ge(s_rd, i * 2 + 2)
                    if g == 4:
                        pe.wait_ge(s_ot, i * 12 + 12)
                    if g >= 4:
                        pe.wait_ge(s_acc_ev, i * 16 + (g - 3))
                    ts, c = slice(t * P, (t + 1) * P), slice(hf * HD, (hf + 1) * HD)
                    products(bank(4 + g % 4, HD), [(OTh[:, k, ts], OTl[:, k, ts], W2h[:, k, c], W2l[:, k, c]) for k in range(KD)], s_p_mm)

            def aggregate(i, first=False, last=False):
                pe.wait_ge(s_hl, i * 16 + 16)
                if not first:
                    pe.wait_ge(s_acc_ev, i * 16)
                for n in range(12):
                    hf, f = n // KD, n % KD
                    d = slice(hf * NH, (hf + 1) * NH)
                    if f == 0:
                        pe.wait_ge(s_P, i * 2 + (hf + 1))
                    if n >= 3:
                        pe.wait_ge(s_y, i * 12 + (n - 2))
                    group(bank(4 + n % 3), [(H[:, s, f * P:(f + 1) * P], PM[:, s, d]) for s in range(NT)], s_agg_mm)
                    if f == 1:
                        pe.wait_ge(s_ps, i * 2 + (hf + 1))
                        if hf:
                            pe.wait_ge(s_rd, i * 2 + hf)
                        group(bank(7), [(ones[:, :], PS)], s_den)
                    if not last and n in (7, 10):
                        k = (7, 10).index(n)
                        row_bc(i * 2 + (H1 + 3 + k), 2 * k)

            aggregate(0, first=True)
            with pe.Fori(1, H1 - 1) as i:
                proj_groups(i - 1)
                aggregate(i)
            proj_groups(H1 - 2)
            aggregate(H1 - 1, last=True)
            pe.wait_ge(s_m2, 1)
            for j in range(NT):
                if j >= 4:
                    pe.wait_ge(s_m2_ev, j - 3)
                for t in range(NT):
                    mm = pe.transpose(psum[:, j % 4, :].bitcast(bf16)[:, t * P:(t + 1) * P], MN2[:, t, j * P:(j + 1) * P], identb[:, :])
                mm.then_inc(s_m2_mm, 1)
            proj_groups(H1 - 1)
            pe.wait_ge(s_m2_ev, NT)
            row_bc(3 * H1 + 1, 0)
            pe.wait_ge(s_mx, H1 + 1)
            row_bc(3 * H1 + 2, 0)
            row_bc(3 * H1 + 3, 2)
            pe.wait_ge(s_P, H1 * 2 + 2)
            pe.wait_ge(s_acc_ev, H1 * 16)
            for t in range(NT):
                for s in range(NT):
                    mm = pe.matmul(psum[:, 0, t:t + 1], PM[:, s, t * P:(t + 1) * P], ones[:, 0:1], start=(s == 0), stop=(s == NT - 1))
            mm.then_inc(s_g2_mm, 1)
            for g in range(16):
                t, hf = g // 2, g % 2
                if g >= 4:
                    pe.wait_ge(s_x1, g - 3)
                group(bank(4 + g % 4, HD), [(PM[:, s, t * P:(t + 1) * P], ACC[:, s, hf * HD:(hf + 1) * HD]) for s in range(NT)], s_g2_mm)


            def turn_rows(n):
                pe.wait_ge(s_ln, NT * (2 * n + 2))
                for g in range(2 * KD):
                    k, hf = g // 2, g % 2
                    if g >= 4:
                        pe.wait_ge(s_xt_ev, 12 * (n + 1) + g - 3)
                    for t in range(4):
                        mm = pe.transpose(psum[:, 4 + g % 4, t * P:(t + 1) * P], LN[:, 4 * hf + t, k * P:(k + 1) * P], ident[:, :])
                    mm.then_inc(s_xt_mm, 1)

            def logits(n):
                pe.wait_ge(s_xt_ev, 12 * (n + 2))
                pe.wait_ge(s_wr, 16 * (n + 1))
                for t in range(NT):
                    for k in range(KD):
                        mm = pe.matmul(psum[:, 0, t * NX:(t + 1) * NX], LT[:, k, t * P:(t + 1) * P], Wr[:, k, :], start=(k == 0), stop=(k == KD - 1))
                mm.then_inc(s_lg, 1)

            turn_rows(0)
            logits(0)
            pe.wait_ge(s_sw, 48)

            def shared_up(j):
                m, hf = j // 2, j % 2
                if j >= 2:
                    pe.wait_ge(s_sact, j - 1)
                for n in range(2):
                    for k in range(KD):
                        mm = pe.matmul(bank(4 + 2 * (j % 2) + n), SW[n][:, k, m * P:(m + 1) * P], LT[:, k, hf * NH:(hf + 1) * NH], start=(k == 0), stop=(k == KD - 1))
                mm.then_inc(s_sg_mm, 1)
            for j in range(6):
                shared_up(j)
            pe.wait_ge(s_rt_in, 1)
            for j in range(3):
                for t in range(NT):
                    src_ = (rt[:, 4, t, :], rt[:, 2, t, :], rt[:, 3, t, :])[j]
                    mm = pe.transpose(psum[0:NX, (0, 2, 0)[j] + t // 4, (t % 4) * P:(t % 4 + 1) * P], src_, ident[:, :])
                    if j == 1 and t == NT - 1:
                        mm.then_inc(s_rt_mm, 1)
                        pe.wait_ge(s_rt_ev, 1)
            mm.then_inc(s_rt_mm, 1)
            pe.wait_ge(s_rt_ev, 3)
            pe.wait_ge(s_sact, 6)
            for n in range(2 * NT):
                t, k = n // 2, n % 2
                if n >= 2:
                    pe.wait_ge(s_rank, n - 1)
                for hf in range(2):
                    mm = pe.matmul(bank(2 * (n % 2) + hf), rowsT[0:NX, 1 + k, t * P:(t + 1) * P], rowsT[0:NX, 0, hf * 512:(hf + 1) * 512], start=True, stop=True)
                mm.then_inc(s_rr_mm, 1)
                t, hf = n // 2, n % 2
                if n >= 4:
                    pe.wait_ge(s_so_ev, n - 3)
                group(bank(4 + n % 4, HD), [(SA[:, m, t * P:(t + 1) * P], SW[2][:, m, hf * HD:(hf + 1) * HD]) for m in range(KM)], s_so_mm)
            pe.wait_ge(s_so_ev, 16)
            pe.wait_ge(s_rank, 16)
            s_ew, s_dr = (s_ew0, s_ew1), (s_dr0, s_dr1)

            def expert(e, i, b, reuse):
                w1, w3, w2 = EW[b]
                pe.wait_ge(s_dr[b], i * 48 + 48)
                for k in range(KD):
                    if k >= 2 or reuse:
                        pe.wait_ge(s_dt_ev, e * 6 + (k - 1))
                    for j, (c0, cn) in enumerate(CB0):
                        mm = pe.transpose(psum[:, k % 2, c0:c0 + cn], DR[b][0:cn, j, k * P:(k + 1) * P], ident[0:cn, 0:cn])
                    mm.then_inc(s_dt_mm, 1)
                pe.wait_ge(s_dt_ev, e * 6 + 6)
                pe.wait_ge(s_ew[b], i * 48 + 48)
                for m in range(KM):
                    if m >= 2 or reuse:
                        pe.wait_ge(s_act, e * 3 + (m - 1))
                    for n, w in enumerate((w1, w3)):
                        for k in range(KD):
                            mm = pe.matmul(bank(2 + 2 * (m % 2) + n, CAP0), w[:, k, m * P:(m + 1) * P], DT[:, k, :], start=(k == 0), stop=(k == KD - 1))
                    mm.then_inc(s_gu_mm, 1)
                pe.wait_ge(s_act, e * 3 + 3)
                for j, (c0, cn) in enumerate(CB0):
                    for hf in range(2):
                        g = 2 * j + hf
                        if g >= 2 or reuse:
                            pe.wait_ge(s_eo_ev, e * 6 + (g - 1))
                        group(psum[0:cn, 6 + hf, 0:HD], [(EA[:, m, c0:c0 + cn], w2[:, m, hf * HD:(hf + 1) * HD]) for m in range(KM)], s_eo_mm)
            expert(0, 0, 0, False)
            expert(1, 0, 1, True)
            with pe.Fori(1, NX // 2) as i:
                expert(i * 2, i, 0, True)
                expert(i * 2 + 1, i, 1, True)

            y0 = kb = 0
            for lay in range(3):
                ft, fo = RIN[lay] // P, ROUT[lay]
                h_ = cut(HN, [NT, RIN[lay]])
                fh = fo // 2

                def half_step(w, half, fill, first=False, counted=False):
                    yb = w * (2 * ft) + (y0 + half * ft)
                    for n in range(ft):
                        if n >= 4:
                            pe.wait_ge(s_y_ev, yb + (n - 3))
                        fill(n, half)
                    pe.wait_ge(s_rwl, w * ft + (kb + ft))
                    pe.wait_ge(s_y_ev, yb + (ft - 1))
                    for g in range(NT):
                        t, hf = g // 2, g % 2
                        if g >= 4 or not first:
                            pe.wait_ge(s_z_ev, w * 16 + (64 * lay + 8 * half + g - 3))
                        if g == 3 and counted:
                            pe.wait_ge(s_cv, w * 2 + (half - 1))
                        ts, c = slice(t * P, (t + 1) * P), slice(hf * fh, (hf + 1) * fh)
                        if g == 0:
                            first_product = [(YTh[:, k, ts], YTl[:, k, ts], RWh[:, k, c], RWl[:, k, c]) for k in range(ft)]
                            for k, (lh, ll, rh, rl) in enumerate(first_product):
                                if k == ft - 1:
                                    pe.wait_ge(s_y_ev, yb + ft)
                                pe.matmul(bank(4, fh), lh, rh, start=(k == 0), stop=False)
                                pe.matmul(bank(4, fh), lh, rl, start=False, stop=False)
                                mm = pe.matmul(bank(4, fh), ll, rh, start=False, stop=(k == ft - 1))
                            mm.then_inc(s_z_mm, 1)
                        else:
                            products(bank(4 + g % 4, fh), [(YTh[:, k, ts], YTl[:, k, ts], RWh[:, k, c], RWl[:, k, c]) for k in range(ft)], s_z_mm)

                def turned(n, half):
                    for t in range(4):
                        mm = pe.transpose(psum[:, n % 4, t * P:(t + 1) * P], h_[:, 4 * half + t, n * P:(n + 1) * P], ident[:, :])
                    mm.then_inc(s_y_mm, 1)

                def summed(n, half):
                    if lay == 0 and n == 3:
                        pe.wait_ge(s_cs, r * 2 + (half + 1))
                        pe.wait_ge(s_z_ev, r * 16 + (16 + 8 * half))
                        for t in range(4):
                            mm = pe.matmul(psum[:, 7, t:t + 1], csum[:, t * P:(t + 1) * P], ones[:, 0:1], start=True, stop=True)
                        mm.then_inc(s_cm, 1)
                    group(bank(n % 4), [(h_[:, s, n * P:(n + 1) * P], AF[:, s, :]) for s in range(NT)], s_y_mm)
                for half in range(2):
                    if lay:
                        pe.wait_ge(s_relu, 16 * (lay - 1) + 8 * (half + 1))
                    elif half == 0:
                        pe.wait_ge(s_hn, 1)
                    half_step(0, half, turned, first=lay == 0 and half == 0)
                with pe.Fori(0, R) as r:
                    for half in range(2):
                        pe.wait_ge(s_af, r * 2 + (lay * R * 2 + half + 1))
                        half_step(r + 1, half, summed, counted=lay == 0)
                y0 += 8 * ft
                kb += 4 * ft

            turn_rows(1)
            logits(1)
            pe.wait_ge(s_rt_in, 2)
            for t in range(NT):
                for j in range(t + 1):
                    mm = pe.matmul(psum[:, 0, t * NX:(t + 1) * NX], ones[:, :] if j < t else before[:, :], rt[:, 2, j, :], start=(j == 0), stop=(j == t))
            mm.then_inc(s_rr_mm, 1)
            s_fw, s_fr = (s_fw0, s_fw1), (s_fr0, s_fr1)
            pe.wait_ge(s_idx, 2)

            def expert1(e, i, b, reuse):
                w1, w2 = GW[b]
                pe.wait_ge(s_fr[b], i * 16 + 16)
                for j in range(2):
                    if reuse:
                        pe.wait_ge(s_ft_ev, e * 2 + (j - 1))
                    for k in range(3):
                        mm = pe.transpose(psum[:, j, k * P:(k + 1) * P], GD[b][:, (3 * j + k) * P:(3 * j + k + 1) * P], ident[:, :])
                    mm.then_inc(s_ft_mm, 1)
                pe.wait_ge(s_ft_ev, e * 2 + 2)
                pe.wait_ge(s_fw[b], i * 64 + 64)
                for m in range(KM):
                    if reuse:
                        pe.wait_ge(s_f1, e * 3 + (m - 2))
                    group(bank(2 + m, C1), [(w1[:, k, m * P:(m + 1) * P], GT[:, k, :]) for k in range(KD)], s_f1_mm)
                pe.wait_ge(s_f1, e * 3 + 3)
                for hf in range(2):
                    if reuse:
                        pe.wait_ge(s_f3, e * 2 + (hf - 1))
                    group(bank(6 + hf, HD), [(GA[:, m, :], w2[:, m, hf * HD:(hf + 1) * HD]) for m in range(KM)], s_f2_mm)
            expert1(0, 0, 0, False)
            expert1(1, 0, 1, True)
            with pe.Fori(1, NX // 2) as i:
                expert1(i * 2, i, 0, True)
                expert1(i * 2 + 1, i, 1, True)

        @block.scalar
        def _(act):
            ch = Chain(act, ach)
            act.wait_ge(s_var, 1)
            act.activation(rstd[:, :], rstd[:, :], ACT.Sqrt).then_inc(s_std, 1)

            def high_half(i, hf, reuse=True):
                act.wait_ge((s_w1a, s_w1b)[hf], i * 16 + 16)
                if reuse:
                    act.wait_ge(s_h_mm, i * 16 + (hf - 1) * 8)
                act.activation(W1h[:, hf], W1r[:, hf], ACT.Copy).then_inc(s_w1h, 1)
            high_half(0, 0, False)
            high_half(0, 1, False)
            for g in range(2 * KD):
                k, hf = g // 2, g % 2
                act.wait_ge(s_xt_mm, g + 1)
                act.activation(XTh[:, k, hf * NH:(hf + 1) * NH], bank(4 + g % 4), ACT.Copy).then_inc(s_xt_hi, 1)

            def features(i, first=False, last=False):
                for g in range(16):
                    hf, t = g // NT, g % NT
                    act.wait_ge(s_h_mm, i * 16 + g + 1)
                    if not first and hf == 0:
                        act.wait_ge(s_dot, i * NT + (t + 1 - NT))
                        act.wait_ge(s_hs[t], i * 16)
                    act.activation(HS[:, t, hf * HD:(hf + 1) * HD], bank(4 + g % 4, HD), ACT.Copy).then_inc(s_h_ev, 1)
                    if hf:
                        act.wait_ge(s_h_ev, i * 16 + g + 1)
                        act.dma_start(hs_d[bass.ds(i, 1), :, t * D:(t + 1) * D].rearrange("o p n -> (o p) n"), HS[:, t, :]).then_inc(s_hs[t], 16)
                    if not last and t == NT - 1:
                        high_half(i + 1, hf)
            features(0, first=True)
            with act.Fori(1, H1 - 1) as i:
                features(i)
            features(H1 - 1, last=True)
            for j in range(NT):
                act.wait_ge(s_mk_mm, j + 1)
                act.activation(MK[:, j, :], psum[:, j % 4, :].bitcast(bf16), ACT.Copy).then_inc(s_mk_ev, 1)

            def probs(i, count):
                act.wait_ge(s_bc, count)
                for n in range(2 * NT):
                    hf, s = n // NT, n % NT
                    if n >= 2:
                        act.wait_ge(s_larger, i * 16 + (n - 1))
                    if n == 0:
                        act.wait_ge(s_at2, i + 1)
                    act.activation(ET[:, n % 2, :], bank(2 + hf), ACT.Exp, bias=cur[:, 1, s:s + 1])
                    act.activation(PM[:, s, hf * NH:(hf + 1) * NH], bank(hf), ACT.Exp, bias=cur[:, 0, s:s + 1]).then_inc(s_exp, 1)

            def head(i, first=False):
                probs(i, i * 2 + (H1 + 2))
                act.wait_ge(s_b1, i * 16 + 16)

                def high(n):
                    hf, f = n // KD, n % KD
                    act.wait_ge(s_zs, i * 12 + (n + 1))
                    act.activation(OTh[:, f, hf * NH:(hf + 1) * NH], Y[:, n % 2, :], ACT.Copy).then_inc(s_oh, 1)
                for n in range(2 * KD):
                    f = n % KD
                    y_ = Y[:, n % 2, :]
                    act.wait_ge(s_y, i * 12 + (n + 1))
                    if n >= 2:
                        act.wait_ge(s_zs, i * 12 + (n - 1))
                    ch.step(act.activation(ET[:, n % 2, :], y_, ACT.Exp, bias=b1c[:, f:f + 1]))
                    ch.sync()
                    act.activation(y_, y_, ACT.Relu, bias=b1c[:, f:f + 1]).then_inc(s_elu, 1)
                    if n < KD:
                        k = n
                        act.wait_ge(s_w2r[k % 2], i * 48 + (k // 2 * 16 + 16))
                        if not first and k == 0:
                            act.wait_ge(s_p_mm, i * 16)
                        act.activation(W2h[:, k, :], W2r[:, k % 2, :], ACT.Copy).then_inc(s_w2h, 1)
                    high(n)

            for t in range(NT):
                act.wait_ge(s_hs[t], H1 * 16)
            head(0, True)
            with act.Fori(1, H1) as i:
                ch.turn(i, 1, 12)
                head(i)
            ch.leave(H1 - 1, 12)
            for j in range(NT):
                act.wait_ge(s_m2_mm, j + 1)
                act.activation(MK2[:, j, :], psum[:, j % 4, :].bitcast(bf16), ACT.Copy).then_inc(s_m2_ev, 1)
            probs(H1, 3 * H1 + 3)

            def root_of_variance(n):
                act.wait_ge(s_var, n + 1)
                act.activation(rstd[:, :], rstd[:, :], ACT.Sqrt).then_inc(s_std, 1)

            def turned_rows(n):
                root_of_variance(n + 1)
                for g in range(2 * KD):
                    k, hf = g // 2, g % 2
                    act.wait_ge(s_xt_mm, 12 * (n + 1) + g + 1)
                    act.activation(LT[:, k, hf * NH:(hf + 1) * NH], bank(4 + g % 4), ACT.Copy).then_inc(s_xt_ev, 1)

            def router_exp(n):
                act.wait_ge(s_ct, n + 1)
                act.activation(rt[:, 0], rt[:, 0], ACT.Exp).then_inc(s_exps, 1)

            turned_rows(0)
            router_exp(0)
            for j in range(6):
                act.wait_ge(s_sg_mm, j + 1)
                if j >= 2:
                    act.wait_ge(s_sact, j - 1)
                act.activation(SG[:, j % 2, :], bank(4 + 2 * (j % 2)), ACT.Silu).then_inc(s_ssilu, 1)
            for j in range(3):
                act.wait_ge(s_rt_mm, 1 + j // 2)
                b0 = 2 * j if j < 2 else 0
                act.activation(rowsT[0:NX, j, :], psum[0:NX, b0:b0 + 2, :].rearrange("p a b -> p (a b)"), ACT.Copy).then_inc(s_rt_ev, 1)

            def expert(e, reuse):
                for k in range(KD):
                    act.wait_ge(s_dt_mm, e * 6 + (k + 1))
                    act.activation(DT[:, k, :], bank(k % 2, CAP0), ACT.Copy).then_inc(s_dt_ev, 1)
                for m in range(KM):
                    act.wait_ge(s_gu_mm, e * 3 + (m + 1))
                    if m >= 2 or reuse:
                        act.wait_ge(s_act, e * 3 + (m - 1))
                    act.activation(EG[:, m % 2, :], bank(2 + 2 * (m % 2), CAP0), ACT.Silu).then_inc(s_silu, 1)
                for j, (c0, cn) in enumerate(CB0):
                    for hf in range(2):
                        g = 2 * j + hf
                        act.wait_ge(s_eo_mm, e * 6 + (g + 1))
                        if reuse and g == 0:
                            act.wait_ge(s_es, e * 48)
                        act.activation(EO[0:cn, j, hf * HD:(hf + 1) * HD], psum[0:cn, 6 + hf, 0:HD], ACT.Copy).then_inc(s_eo_ev, 1)
                    act.wait_ge(s_eo_ev, e * 6 + (2 * j + 2))
                    act.dma_start(eout0_d[bass.ds(e * CAP0 + c0, cn), :], EO[0:cn, j, :]).then_inc(s_es, 16)
            expert(0, False)
            with act.Fori(1, NX) as e:
                expert(e, True)

            def relus(lay, groups):
                fo = ROUT[lay]
                o_, fh = cut(HN, [NT, fo]), fo // 2
                for g in groups:
                    t, hf = g // 2, g % 2
                    act.wait_ge(s_z_ev, 64 * lay + 48 + g + 1)
                    act.activation(o_[:, t, hf * fh:(hf + 1) * fh], cut(RA, [NT, fo])[:, t, hf * fh:(hf + 1) * fh], ACT.Relu).then_inc(s_relu, 1)
            y0 = kb = 0
            slot0 = [0, 0]
            for lay in range(3):
                ft, fo = RIN[lay] // P, ROUT[lay]
                fh = fo // 2
                slots_ = [-(-ft // 2), ft // 2]

                def weights(w, first=False, rows=range(ft)):
                    for k in rows:
                        act.wait_ge(s_rw[k % 2], w * (16 * slots_[k % 2]) + 16 * (slot0[k % 2] + k // 2 + 1))
                        if k == 0 and not first:
                            act.wait_ge(s_z_mm, w * 16 + 64 * lay)
                        act.activation(RWh[:, k, 0:fo], RWr[:, k % 2, 0:fo], ACT.Copy).then_inc(s_rwh, 1)

                def highs(w, half, ahead=lambda n: None):
                    for n in range(ft):
                        ahead(n)
                        act.wait_ge(s_y_mm, w * (2 * ft) + (y0 + half * ft + n + 1))
                        act.activation(YTh[:, n, :], bank(n % 4), ACT.Copy).then_inc(s_yh, 1)

                def widen(w, half):
                    if lay == 0:
                        if half or not isinstance(w, int):
                            act.wait_ge(s_cs, w * 2 + (half - 2))
                    elif half == 0 and isinstance(w, int):
                        act.wait_ge(s_cs, 2 * R)
                    if half == 0:
                        act.wait_ge(s_ar, w * 16 + lay * R * 16)
                    act.wait_ge(s_y_mm, w * (2 * ft) + (y0 + half * ft))
                    act.activation(AF, AR[:, :, half * NH:(half + 1) * NH], ACT.Copy).then_inc(s_af, 1)

                def relation(w):
                    widen(w, 0)
                    highs(w, 0, lambda n: weights(w, rows=[n]))
                    widen(w, 1)
                    highs(w, 1)
                if lay == 0:
                    weights(0, first=True)
                    root_of_variance(2)
                    highs(0, 0)
                else:
                    weights(0, rows=range(2))
                    highs(0, 0, lambda n: weights(0, rows=[n + 2] if n + 2 < ft else []))
                    relus(lay - 1, range(8, 16))
                highs(0, 1)
                relation(1)
                with act.Fori(2, 1 + R) as w:
                    relation(w)
                y0 += 8 * ft
                for p_ in range(2):
                    slot0[p_] += 4 * slots_[p_]
                if lay < 2:
                    act.wait_ge(s_y_mm, y0)
                    relus(lay, range(8))

            root_of_variance(3)
            for g in range(2 * KD):
                k, hf = g // 2, g % 2
                act.wait_ge(s_xt_mm, 24 + g + 1)
                act.activation(LT[:, k, hf * NH:(hf + 1) * NH], bank(4 + g % 4), ACT.Copy).then_inc(s_xt_ev, 1)
            router_exp(1)
            s_fw = (s_fw0, s_fw1)

            def expert1(e, i, b, reuse):
                for j in range(2):
                    act.wait_ge(s_ft_mm, e * 2 + (j + 1))
                    act.activation(GT[:, 3 * j:3 * j + 3, :].rearrange("p a b -> p (a b)"), bank(j, 3 * P), ACT.Copy).then_inc(s_ft_ev, 1)
                act.wait_ge(s_fw[b], i * 64 + 64)
                for m in range(KM):
                    act.wait_ge(s_f1_mm, e * 3 + (m + 1))
                    act.activation(GA[:, m, :], bank(2 + m, C1), ACT.Gelu_apprx_tanh, bias=gb1[b][:, m:m + 1]).then_inc(s_f1, 1)
                for hf in range(2):
                    act.wait_ge(s_f3, e * 2 + (hf + 1))
                    g_ = GO[:, b, hf * HD:(hf + 1) * HD]
                    act.activation(g_, g_, ACT.Gelu_apprx_tanh).then_inc(s_f2, 1)
                act.wait_ge(s_f2, e * 2 + 2)
                act.dma_start(eout1_d[bass.ds(e * C1, C1), :], GO[:, b, :]).then_inc((s_fs0, s_fs1)[b], 16)
            expert1(0, 0, 0, False)
            expert1(1, 0, 1, True)
            with act.Fori(1, NX // 2) as i:
                expert1(i * 2, i, 0, True)
                expert1(i * 2 + 1, i, 1, True)

        @block.vector
        def _(dve):
            ch = Chain(dve, dch)
            step, sync = ch.step, ch.sync

            def norm_stats(xv, t):
                for h in range(2):
                    step(dve.bn_stats(stats[:, t, h, :], xv[:, t, h * HD:(h + 1) * HD]))
                sync()
                step(dve.bn_aggr(mv[:, t, :], stats[:, t, :, :]))

            def normalize(xv, o_):
                for t in range(NT):
                    norm_stats(xv, t)
                sync()
                dve.tensor_scalar(rstd[:, :], mv[:, :, 1], EPS, None, ADD).then_inc(s_var, 1)

            dve.wait_ge(s_edges, 48)
            e_src, e_dst, e_typ = (edges[:, k, :] for k in range(3))
            step(dve.tensor_scalar(ework[:, 0, :], e_src, 7, None, ALU.logical_shift_right))
            step(dve.tensor_scalar(ework[:, 1, :], e_src, P - 1, 10, ALU.bitwise_and, ALU.logical_shift_left))
            step(dve.tensor_scalar(ework[:, 3, :], e_typ, 3, None, ALU.logical_shift_left))
            sync()
            step(dve.tensor_tensor(code, ework[:, 1, :], e_dst, ALU.bitwise_or))
            step(dve.tensor_tensor(ework[:, 2, :], ework[:, 3, :], ework[:, 0, :], ALU.bitwise_or))
            sync()
            step(dve.tensor_copy(keyf, ework[:, 2, :]))
            sync()
            dve.wait_ge(s_const, 5)
            step(dve.tensor_tensor(onehot, keyf.unsqueeze(1).to_broadcast([P, NBK, EC]),
                                   iota[:, 0:NBK].unsqueeze(2).to_broadcast([P, NBK, EC]), ALU.is_equal))
            step(dve.memset(bk[:, 0, 0:1], 0.0))
            sync()
            step(dve.tensor_tensor_scan(running.rearrange("p b c -> p (b c)"),
                                        ones[:, 0:1].to_broadcast([P, NBK * EC]),
                                        onehot.rearrange("p b c -> p (b c)"), 0.0, MULT, ADD))
            sync()
            step(dve.tensor_copy(bk[:, 0, 1:NBK + 1], running[:, :, EC - 1]))
            sync()
            dve.tensor_tensor(bk[:, 2, 0:NBK], bk[:, 0, 1:NBK + 1], bk[:, 0, 0:NBK], SUB).then_inc(s_cnt, 1)
            dve.wait_ge(s_tot, 2)
            step(dve.tensor_scalar(bki, bank(1, NBK), float(P - 1), None, ADD))
            sync()
            step(dve.tensor_scalar(bki, bki, 7, None, ALU.logical_shift_right))
            sync()
            step(dve.tensor_copy(bk[:, 3, 0:NBK], bki))
            sync()
            step(dve.tensor_tensor_scan(bk[:, 4, 0:NBK], ones[:, 0:1].to_broadcast([P, NBK]), bk[:, 3, 0:NBK], 0.0, MULT, ADD))
            step(dve.tensor_tensor(bk[:, 5, 0:NBK], bank(0, NBK), bk[:, 0, 0:NBK], SUB))
            sync()
            step(dve.tensor_tensor(bk[:, 6, 0:NBK], bk[:, 4, 0:NBK], bk[:, 3, 0:NBK], SUB))
            sync()
            step(dve.scalar_tensor_tensor(bk[:, 7, 0:NBK], bk[:, 6, 0:NBK], float(P), bk[:, 5, 0:NBK], MULT, ADD))
            sync()
            step(dve.tensor_scalar(bk[:, 8, 0:NBK], bk[:, 7, 0:NBK], -1.0, None, ADD))
            sync()
            step(dve.tensor_tensor(running, running, bk[:, 8, 0:NBK].unsqueeze(2).to_broadcast([P, NBK, EC]), ADD))
            sync()
            step(dve.tensor_tensor(running, running, onehot, MULT))
            sync()
            step(dve.tensor_reduce(slotf, running.rearrange("p b c -> p c b"), AX.X, ADD))
            sync()
            step(dve.tensor_copy(sloti[:, 0, :], slotf))
            sync()
            step(dve.tensor_scalar(sloti[:, 1, :], sloti[:, 0, :], 7, None, ALU.logical_shift_right))
            step(dve.tensor_scalar(sloti[:, 2, :], sloti[:, 0, :], P - 1, None, ALU.bitwise_and))
            sync()
            dve.scalar_tensor_tensor(row, sloti[:, 2, :], float(NCH), sloti[:, 1, :], MULT, ADD).then_inc(s_row, 1)
            step(dve.tensor_tensor(cmp[0:1], iota[0:1, 0:NCH].unsqueeze(2).to_broadcast([1, NCH, NBK]),
                                   bk[0:1, 4, 0:NBK].unsqueeze(1).to_broadcast([1, NCH, NBK]), ALU.is_ge))
            sync()
            step(dve.tensor_reduce(boff[0:1], cmp[0:1], AX.X, ADD))
            sync()
            step(dve.tensor_scalar(boffi[0:1], boff[0:1], float(NBK - 1), float(N), MIN, MULT))
            step(dve.tensor_copy(iotah, iota))
            step(dve.tensor_copy(identb[:, :], ident[:, :]))
            dve.wait_ge(s_x, 16)
            normalize(XL, XL)
            dve.wait_ge(s_std, 1)
            step(dve.reciprocal(rstd[:, :], rstd[:, :]))
            sync()
            for t in range(NT):
                dve.tensor_scalar(XL[:, t, :], XL[:, t, :], mv[:, t, 0:1], rstd[:, t:t + 1], SUB, MULT).then_inc(s_ln, 1)
            step(dve.memset(recf, -1.0))
            dve.wait_ge(s_zero, 16 * (NX * (CAP0 + C1) // P))
            sync()
            for n in range(2):
                dve.memset(A_r[:, n * NBK * N // 2:(n + 1) * NBK * N // 2], 0).then_inc(s_added, 1)
            for g in range(2 * KD):
                k, hf = g // 2, g % 2
                d = slice(hf * NH, (hf + 1) * NH)
                dve.wait_ge(s_xt_hi, g + 1)
                dve.tensor_tensor(XTl[:, k, d], bank(4 + g % 4), XTh[:, k, d].bitcast(fp32), SUB).then_inc(s_xt_ev, 1)

            def carry():
                sync()
                step(dve.tensor_copy(mx[:, 3, 0:1], ones[:, 0:1]))

            def vector_of(i, k):
                return VA[:, bass.ds(i * 4 * NT + k * NT, NT)]

            def dots(i, t, first=False):
                dve.wait_ge(s_h_ev, i * 16 + (t + 9))
                if t == 0:
                    dve.wait_ge(s_a, i * 32 + 32)
                if t or not first:
                    dve.wait_ge(s_dot, i * NT + t)
                step(dve.tensor_tensor_reduce(dots_junk, HS[:, t, :], a_bc[:, 0, :], 1.0, 0.0, MULT, ADD, alpha[:, 0, t:t + 1]))
                sync()
                dve.tensor_tensor_reduce(dots_junk, HS[:, t, :], a_bc[:, 1, :], 1.0, 0.0, MULT, ADD, alpha[:, 1, t:t + 1]).then_inc(s_dot, 1)
                if t == NT - 1:
                    dve.wait_ge(s_dot, i * NT + NT)
                    carry()
                    step(dve.tensor_copy(vector_of(i, 0), alpha[:, 0, :]))
                    step(dve.tensor_copy(vector_of(i, 3), alpha[:, 1, :]))
                    sync()
            for i in range(2):
                for t in range(NT):
                    dots(i, t, i == 0)
            dve.wait_ge(s_recs, 16)
            step(dve.tensor_scalar(recs[:, 1, :], recs[:, 0, :], 10, None, ALU.arith_shift_right))
            step(dve.tensor_scalar(recs[:, 2, :], recs[:, 0, :], N - 1, None, ALU.bitwise_and))
            sync()
            step(dve.tensor_copy(recf[:, :, 0:NCH], recs[:, 1:3, :]))
            sync()

            def hots(c, par, reuse=True):
                if reuse:
                    dve.wait_ge(s_pair, c - 1)
                dve.tensor_scalar(S1[:, par, :], iotah[:, 0:P], recf[:, 0, bass.ds(c, 1)], None, ALU.is_equal)
                dve.tensor_scalar(D1[:, par, :], iotah, recf[:, 1, bass.ds(c, 1)], None, ALU.is_equal).then_inc(s_hot, 1)

            def add(c, par):
                off = dve.value_load(boffi[0:1, bass.ds(c, 1)], min_val=0, max_val=(NBK - 1) * N)
                dve.wait_ge(s_pair, c + 1)
                dve.wait_ge(s_added, c + 2)
                part_ = A_r[:, bass.ds(off, N)]
                dve.tensor_tensor(part_, psum[:, 2 * par:2 * par + 2, :].rearrange("p a b -> p (a b)"), part_, ADD).then_inc(s_added, 1)
            hots(0, 0, False)
            hots(1, 1, False)
            for t in range(NT):
                dots(2, t)
            PERD = NT + 3
            with dve.Fori(3, H1) as i:
                ch.turn(i, 3, PERD)
                for j in range(16):
                    for par in range(2):
                        c = (i - 3) * 32 + (2 * j + par)
                        add(c, par)
                        hots((i - 3) * 32 + (2 * j + par + 2), par)
                    if j >= 9:
                        dots(i, j - 9)
                dots(i, NT - 1)
            ch.leave(H1 - 3, PERD)
            dve.wait_ge(s_added, NCH + 2)
            ATf = AT.rearrange("p a b -> p (a b)")
            dve.wait_ge(s_h_mm, H1 * 16)
            dve.wait_ge(s_pair, NCH)
            dve.wait_ge(s_hot, NCH + 2)
            step(dve.tensor_tensor(ATf, A_r[:, 0:NT * N], A_r[:, NT * N:2 * NT * N], ADD))
            sync()
            step(dve.tensor_tensor(ATf, ATf, A_r[:, 2 * NT * N:3 * NT * N], ADD))
            sync()
            dve.tensor_scalar(MN.rearrange("p a b -> p (a b)"), ATf, 0.0, NEG, ALU.is_equal, MULT).then_inc(s_mn, 1)

            def on_diagonal(v, count):
                if count is not None:
                    dve.wait_ge(s_bc, count)
                carry()
                dve.tensor_tensor(DG.rearrange("p (t n) -> p t n", t=NT), ident[:, :].unsqueeze(1).to_broadcast([P, NT, P]),
                                  v.unsqueeze(2).to_broadcast([P, NT, P]), MULT).then_inc(s_diag, 1)

            def maxima(i, b, mk, junk_, count, s0=0):
                carry()
                step(dve.tensor_copy(alpha[:, 0, :], vector_of(i, 0)))
                step(dve.tensor_copy(alpha[:, 1, :], vector_of(i, 3)))
                dve.wait_ge(s_bc, count)
                srow = psum[:, b:b + 2, :].rearrange("p a b -> p (a b)")
                for t in range(NT):
                    sync()
                    step(dve.tensor_copy(mx[:, 3, t:t + 1], ones[:, 0:1]))
                    step(dve.tensor_tensor_reduce(junk_, mk[:, t, :], srow, 1.0, 3 * NEG, ADD, MAX, mx[:, 0, t:t + 1]))
                sync()
                step(dve.tensor_tensor(mx[:, 1, :], mx[:, 0, :], alpha[:, 1, :], ADD))
                sync()
                step(dve.scalar_tensor_tensor(mx[:, 2, :], mx[:, 1, :], 0.2, mx[:, 1, :], MULT, MAX))
                carry()
                step(dve.tensor_scalar(vector_of(i, 1), alpha[:, 0, :], 0.2, None, MULT))
                step(dve.tensor_tensor(vector_of(i, 2), alpha[:, 1, :], mx[:, 2, :], SUB))
                step(dve.scalar_tensor_tensor(mx[:, 1, :], alpha[:, 1, :], 0.2, mx[:, 2, :], MULT, SUB))
                carry()
                dve.tensor_copy(vector_of(i, 3), mx[:, 1, :]).then_inc(s_mx, 1)
                dve.wait_ge(s_mx, i + 1)

            dve.wait_ge(s_mk_ev, NT)
            on_diagonal(vector_of(0, 0), None)
            PERM = 2 + 2 * NT + 5 + 4
            with dve.Fori(0, H1 // 2 - 1) as i:
                ch.turn(i, 0, 2 * PERM)
                for b in range(2):
                    on_diagonal(vector_of(i * 2 + (b + 1), 0), i * 2 + (b + 1))
                    maxima(i * 2 + b, 2 * b, MK, junk, i * 2 + (b + 1))
            ch.leave(H1 // 2 - 1, 2 * PERM)
            on_diagonal(vector_of(H1 - 1, 0), H1 - 1)
            maxima(H1 - 2, 0, MK, junk, H1 - 1)
            maxima(H1 - 1, 2, MK, junk, H1)
            dve.wait_ge(s_spill, 16 * R)

            def set_current(i):
                carry()
                dve.tensor_copy(cur[:, :, :].rearrange("p a b -> p (a b)"), VA[:, bass.ds(i * 4 * NT, 2 * NT)]).then_inc(s_at2, 1)

            def rows_of(i, k):
                on_diagonal(vector_of(i, 2 + k), i * 2 + (H1 + k))
            rows_of(0, 0)
            rows_of(0, 1)
            set_current(0)

            def acc_evac(i, g, first):
                hf, t = g // NT, g % NT
                a_ = ACC[:, t, hf * HD:(hf + 1) * HD]
                dve.wait_ge(s_p_mm, i * 16 + (g + 1))
                if first:
                    dve.tensor_copy(a_, bank(4 + g % 4, HD)).then_inc(s_acc_ev, 1)
                else:
                    dve.tensor_tensor(a_, bank(4 + g % 4, HD), a_, ADD).then_inc(s_acc_ev, 1)

            def attention(i, evac):
                for n in range(2 * NT):
                    hf, s = n // NT, n % NT
                    p_ = PM[:, s, hf * NH:(hf + 1) * NH]
                    dve.wait_ge(s_exp, i * 16 + (n + 1))
                    dve.scalar_tensor_tensor(p_, p_, 1.0, ET[:, n % 2, :], MIN, MAX).then_inc(s_larger, 1)
                    evac(n)
                    if s == NT - 1:
                        d = slice(hf * NH, (hf + 1) * NH)
                        dve.wait_ge(s_larger, i * 16 + (n + 1))
                        dve.scalar_tensor_tensor(PM[:, :, d], PM[:, :, d], 1.0, AT[:, :, d], MIN, MULT).then_inc(s_P, 1)

            def head(i, first=False, second=False, last=False):
                attention(i, lambda n: None if first else acc_evac(i - 1, n, second))

                def fix(n):
                    dve.wait_ge(s_elu, i * 12 + (n + 1))
                    dve.tensor_scalar(ET[:, n % 2, :], ET[:, n % 2, :], 1.0, -1.0, MIN, ADD).then_inc(s_efix, 1)
                for n in range(2 * KD):
                    hf, f = n // KD, n % KD
                    if f == 0:
                        if hf or not first:
                            dve.wait_ge(s_y, i * 12 + n)
                        dve.wait_ge(s_den, i * 2 + (hf + 1))
                        step(dve.tensor_scalar(RD, bank(7), 1e-16, None, ADD))
                        sync()
                        dve.reciprocal(RD, RD).then_inc(s_rd, 1)
                        dve.wait_ge(s_rd, i * 2 + (hf + 1))
                    dve.wait_ge(s_agg_mm, i * 12 + (n + 1))
                    if n >= 2 or not first:
                        dve.wait_ge(s_ot, i * 12 + (n - 1))
                    dve.tensor_tensor(Y[:, n % 2, :], bank(4 + n % 3), RD, MULT).then_inc(s_y, 1)
                    fix(n)
                    if not last and n == 5:
                        rows_of(i + 1, 0)
                    if not last and n == 9:
                        rows_of(i + 1, 1)
                        set_current(i + 1)

            head(0, first=True)
            head(1, second=True)
            with dve.Fori(2, H1 - 1) as i:
                ch.turn(i, 2, 5)
                head(i)
            ch.leave(H1 - 3, 5)
            head(H1 - 1, last=True)
            dve.wait_ge(s_agg_mm, H1 * 12)
            dve.tensor_scalar(MN2.rearrange("p a b -> p (a b)"), ATf, 0.0, NEG, ALU.is_equal, MULT).then_inc(s_m2, 1)
            for g in range(16):
                acc_evac(H1 - 1, g, False)
            dve.wait_ge(s_acc_ev, H1 * 16)
            dve.wait_ge(s_a, H1 * 32 + 32)
            for k in range(2):
                for t in range(NT):
                    step(dve.tensor_tensor_reduce(junk2[:, 0:D], ACC[:, t, :], a2_bc[:, k, :], 1.0, 0.0, MULT, ADD, alpha[:, k, t:t + 1]))
                    sync()
            step(dve.tensor_copy(vector_of(H1, 0), alpha[:, 0, :]))
            step(dve.tensor_copy(vector_of(H1, 3), alpha[:, 1, :]))
            sync()
            on_diagonal(vector_of(H1, 0), 3 * H1)
            dve.wait_ge(s_m2_ev, NT)
            maxima(H1, 0, MK2, junk2, 3 * H1 + 1)
            on_diagonal(vector_of(H1, 2), 3 * H1 + 1)
            on_diagonal(vector_of(H1, 3), 3 * H1 + 2)
            set_current(H1)
            attention(H1, lambda n: None)
            dve.wait_ge(s_g2_mm, 1)
            step(dve.tensor_scalar(rd2[:, :], psum[:, 0, 0:NT], 1e-16, None, ADD))
            sync()
            step(dve.reciprocal(rd2[:, :], rd2[:, :]))
            sync()
            dve.wait_ge(s_xr, 32)
            for t in range(NT):
                step(dve.tensor_tensor(XN[:, t, :], XN[:, t, :], b2_bc, ADD))
            sync()
            for g in range(16):
                t, hf = g // 2, g % 2
                x_ = XN[:, t, hf * HD:(hf + 1) * HD]
                dve.wait_ge(s_g2_mm, g + 2)
                dve.scalar_tensor_tensor(x_, bank(4 + g % 4, HD), rd2[:, t:t + 1], x_, MULT, ADD).then_inc(s_x1, 1)

            def layernorm(n, to, width):
                sync()
                for t in range(NT):
                    norm_stats(XN, t)
                sync()
                dve.wait_ge(s_ln, NT * n)
                dve.tensor_scalar(rstd[:, :], mv[:, :, 1], EPS, None, ADD).then_inc(s_var, 1)
                dve.wait_ge(s_std, n + 1)
                step(dve.reciprocal(rstd[:, :], rstd[:, :]))
                sync()
                for t in range(NT):
                    dve.tensor_scalar(to[:, t, 0:D], XN[:, t, :], mv[:, t, 0:1], rstd[:, t:t + 1], SUB, MULT).then_inc(s_ln, 1)

            def over_experts(v):
                return v.unsqueeze(2).to_broadcast([P, NT, NX])

            def router_probs(n):
                dve.wait_ge(s_lg, n + 1)
                step(dve.tensor_copy(rt[:, 0], psum[:, 0, 0:NT * NX].rearrange("p (a b) -> p a b", a=NT)))
                sync()
                step(dve.tensor_reduce(rk[:, 0, 0], rt[:, 0], AX.X, MAX))
                sync()
                dve.tensor_tensor(rt[:, 0], rt[:, 0], over_experts(rk[:, 0, 0]), SUB).then_inc(s_ct, 1)
                dve.wait_ge(s_exps, n + 1)
                step(dve.tensor_reduce(rk[:, 0, 1], rt[:, 0], AX.X, ADD))
                sync()
                step(dve.reciprocal(rk[:, 0, 1], rk[:, 0, 1]))
                sync()
                step(dve.tensor_tensor(rt[:, 1], rt[:, 0], over_experts(rk[:, 0, 1]), MULT))
                sync()
                for t in range(NT):
                    step(dve.max(m8[:, t, :], rt[:, 1, t, :]))
                sync()
                for t in range(NT):
                    step(dve.max_index(ix[:, t, :], m8[:, t, :], rt[:, 1, t, :]))
                sync()

            def one_hot(k):
                step(dve.tensor_copy(rk[:, 2, k], ix[:, :, k]))
                sync()
                step(dve.tensor_tensor(rt[:, 2 + k], iota8[:, :].unsqueeze(1).to_broadcast([P, NT, NX]), over_experts(rk[:, 2, k]), ALU.is_equal))

            def places(k, rank, cap, low):
                w_, e_ = rk[:, 1, k], rk[:, 2, k]
                step(dve.tensor_scalar(rk[:, 5, k], rank, float(cap), None, ALU.is_lt))
                step(dve.scalar_tensor_tensor(rk[:, 6, k], e_, float(cap), rank, MULT, ADD))
                sync()
                step(dve.tensor_scalar(rk[:, 7, k], rk[:, 5, k], -1e6, 1e6, MULT, ADD))
                step(dve.tensor_tensor(idx[:, 1, k, :], rk[:, 6, k], rk[:, 5, k], MULT))
                step(dve.tensor_tensor(rk[:, 8, k], w_, rk[:, 5, k], MULT))
                sync()
                return step(dve.tensor_tensor(idx[:, 0, k, :], rk[:, 6, k], rk[:, 7, k], ADD))

            dve.wait_ge(s_x1, 16)
            layernorm(1, LN, D)
            router_probs(0)
            for k in range(2):
                one_hot(k)
            step(dve.tensor_tensor(rk[:, 3, 0], m8[:, :, 0], m8[:, :, 1], ADD))
            sync()
            step(dve.tensor_scalar(rk[:, 3, 0], rk[:, 3, 0], 1e-9, None, MAX))
            sync()
            step(dve.reciprocal(rk[:, 3, 1], rk[:, 3, 0]))
            sync()
            for k in range(2):
                step(dve.tensor_tensor(rk[:, 1, k], m8[:, :, k], rk[:, 3, 1], MULT))
            sync()
            for k in range(2):
                step(dve.tensor_tensor(rt[:, 5 + k], rt[:, 2 + k], over_experts(rk[:, 1, k]), MULT))
            sync()
            step(dve.tensor_tensor(rt[:, 7], rt[:, 2], rt[:, 3], ADD))
            step(dve.tensor_tensor(rt[:, 8], rt[:, 5], rt[:, 6], ADD))
            sync()
            step(dve.tensor_scalar(rt[:, 9], rt[:, 7], -1.0, None, ADD))
            sync()
            dve.tensor_tensor(rt[:, 4], rt[:, 8], rt[:, 9], ADD).then_inc(s_rt_in, 1)
            for j in range(6):
                m, hf = j // 2, j % 2
                dve.wait_ge(s_ssilu, j + 1)
                dve.tensor_tensor(SA[:, m, hf * NH:(hf + 1) * NH], SG[:, j % 2, :], bank(5 + 2 * (j % 2)), MULT).then_inc(s_sact, 1)
            dve.wait_ge(s_tri, 1)
            for n in range(2 * NT):
                t, k = n // 2, n % 2
                dve.wait_ge(s_rr_mm, n + 1)
                r_ = psum[:, 2 * (n % 2):2 * (n % 2) + 2, :].rearrange("p a b -> p (a b)")
                sync()
                step(dve.tensor_scalar(rjunk, r_, rk[:, 1, k, t:t + 1], 0.0, ALU.is_gt, ADD, accum_out=rk[:, 4, k, t:t + 1]))
                sync()
                if n:
                    dve.wait_ge(s_rank, n)
                dve.scalar_tensor_tensor(rjunk, r_, rk[:, 1, k, t:t + 1], earlier[:, N - P - t * P:2 * N - P - t * P], ALU.is_equal, MULT,
                                         accum_out=rk[:, 9, k, t:t + 1]).then_inc(s_rank, 1)
                dve.wait_ge(s_rank, n + 1)
                t, hf = n // 2, n % 2
                x_ = XN[:, t, hf * HD:(hf + 1) * HD]
                dve.wait_ge(s_so_mm, n + 1)
                dve.tensor_tensor(x_, bank(4 + n % 4, HD), x_, ADD).then_inc(s_so_ev, 1)
            for k in range(2):
                step(dve.tensor_tensor(rk[:, 10, k], rk[:, 4, k], rk[:, 9, k], ADD))
                sync()
                last = places(k, rk[:, 10, k], CAP0, 0)
            sync()
            step(dve.tensor_copy(rk[:, 11, 0], rk[:, 10, 0]))
            sync()
            dve.tensor_copy(rk[:, 11, 1], rk[:, 10, 0]).then_inc(s_idx, 1)

            def expert(e):
                for m in range(KM):
                    dve.wait_ge(s_silu, e * 3 + (m + 1))
                    dve.tensor_tensor(EA[:, m, :], EG[:, m % 2, :], bank(3 + 2 * (m % 2), CAP0), MULT).then_inc(s_act, 1)
            expert(0)
            with dve.Fori(1, NX) as e:
                expert(e)
            s_ga = (s_ga0, s_ga1, s_ga2, s_ga3)

            def combine(n, k, t, base, gathered):
                dve.wait_ge(s_ga[n % 4], 16 * (gathered + n // 4 + 1))
                if n or base:
                    dve.wait_ge(s_comb, base + n)
                dve.scalar_tensor_tensor(XN[:, t, :], GR[n % 4], rk[:, 8, k, t:t + 1], XN[:, t, :], MULT, ADD).then_inc(s_comb, 1)
            dve.wait_ge(s_so_ev, 16)
            for n in range(2 * NT):
                combine(n, n % 2, n // 2, 0, 0)
            dve.wait_ge(s_comb, 2 * NT)

            h_ = cut(HN, [NT, RIN[0]])
            dve.wait_ge(s_emb, 32)
            step(dve.tensor_copy(ntypef[:, :], ntype[:, :]))
            layernorm(2, h_, RIN[0])
            for j in range(R):
                step(dve.tensor_scalar(mx[:, j, :], ntypef[:, :], float(j), None, ALU.is_equal))
            sync()
            for j in range(R):
                for t in range(NT):
                    e_ = h_[:, t, D:D + TD]
                    if j == 0:
                        step(dve.tensor_scalar(e_, emb[:, j, :], mx[:, j, t:t + 1], None, MULT))
                    else:
                        step(dve.scalar_tensor_tensor(e_, emb[:, j, :], mx[:, j, t:t + 1], e_, MULT, ADD))
                sync()
            dve.wait_ge(s_ln, 3 * NT)
            dve.tensor_copy(rd2[:, :], ntypef[:, :]).then_inc(s_hn, 1)
            y0 = 0
            for lay in range(3):
                ft, fo = RIN[lay] // P, ROUT[lay]
                fh = fo // 2
                a_ = cut(RA, [NT, fo])

                def lows(w, half):
                    for n in range(ft):
                        dve.wait_ge(s_yh, w * (2 * ft) + (y0 + half * ft + n + 1))
                        dve.tensor_tensor(YTl[:, n, :], bank(n % 4), YTh[:, n, :].bitcast(fp32), SUB).then_inc(s_y_ev, 1)
                for half in range(2):
                    lows(0, half)
                    dve.wait_ge(s_rb, 16 * (lay + 1))
                    for g in range(8 * half, 8 * half + 8):
                        t, hf = g // 2, g % 2
                        dve.wait_ge(s_z_mm, 64 * lay + g + 1)
                        if lay:
                            dve.wait_ge(s_relu, 16 * (lay - 1) + 8 * (half + 1))
                        dve.tensor_tensor(a_[:, t, hf * fh:(hf + 1) * fh], bank(4 + g % 4, fh), bias_bc[:, hf * fh:(hf + 1) * fh], ADD).then_inc(s_z_ev, 1)
                PERR = 8 if lay == 0 else 2
                with dve.Fori(0, R) as r:
                    ch.turn(r, 0, PERR)
                    dve.wait_ge(s_z_ev, r * 16 + (64 * lay + 16))
                    if lay:
                        carry()
                        step(dve.tensor_copy(inv_r, inv[:, bass.ds(r * NT, NT)]))
                    for half in range(2):
                        i_ = inv_r[:, 4 * half:4 * half + 4]
                        if lay == 0:
                            c_ = psum[:, 7, 0:4]
                            dve.wait_ge(s_cm, r * 2 + (half + 1))
                            step(dve.tensor_scalar(cwork[:, 0, :], c_, 1.0, None, MAX))
                            sync()
                            step(dve.reciprocal(cwork[:, 1, :], cwork[:, 0, :]))
                            sync()
                            dve.scalar_tensor_tensor(i_, c_, 1.0, cwork[:, 1, :], MIN, MULT).then_inc(s_cv, 1)
                            dve.wait_ge(s_cv, r * 2 + (half + 1))
                            carry()
                            step(dve.tensor_copy(inv[:, bass.ds(r * NT + 4 * half, 4)], i_))
                        lows(r + 1, half)
                        sync()
                        for g in range(8 * half, 8 * half + 8):
                            t, hf = g // 2, g % 2
                            o_ = a_[:, t, hf * fh:(hf + 1) * fh]
                            dve.wait_ge(s_z_mm, r * 16 + (64 * lay + 16 + g + 1))
                            dve.wait_ge(s_z_ev, r * 16 + (64 * lay + g + 1))
                            dve.scalar_tensor_tensor(o_, bank(4 + g % 4, fh), inv_r[:, t:t + 1], o_, MULT, ADD).then_inc(s_z_ev, 1)
                ch.leave(R, PERR)
                y0 += 8 * ft
            dve.wait_ge(s_z_ev, 3 * 64)
            for g in range(16):
                t, hf = g // 2, g % 2
                x_ = XN[:, t, hf * HD:(hf + 1) * HD]
                dve.scalar_tensor_tensor(x_, cut(13312, [NT, D])[:, t, hf * HD:(hf + 1) * HD], 0.0, x_, MAX, ADD).then_inc(s_x3, 1)

            dve.wait_ge(s_x3, 16)
            layernorm(3, LN, D)
            router_probs(1)
            one_hot(0)
            step(dve.tensor_copy(rk[:, 1, 0], m8[:, :, 0]))
            sync()
            dve.tensor_copy(rk[:, 3, 0], rk[:, 1, 0]).then_inc(s_rt_in, 1)
            dve.wait_ge(s_rr_mm, 2 * NT + 1)
            step(dve.tensor_tensor(rt[:, 5], psum[:, 0, 0:NT * NX].rearrange("p (a b) -> p a b", a=NT), rt[:, 2], MULT))
            sync()
            step(dve.tensor_reduce(rk[:, 4, 0], rt[:, 5], AX.X, ADD))
            sync()
            step(dve.tensor_scalar(rk[:, 10, 0], rk[:, 4, 0], 1.0, None, ADD))
            sync()
            places(0, rk[:, 10, 0], C1, 0)
            sync()
            dve.tensor_copy(rk[:, 11, 0], rk[:, 10, 0]).then_inc(s_idx, 1)
            s_fw = (s_fw0, s_fw1)

            def expert1(e, i, b, reuse):
                dve.wait_ge(s_fw[b], i * 64 + 64)
                for hf in range(2):
                    dve.wait_ge(s_f2_mm, e * 2 + (hf + 1))
                    if reuse and hf == 0:
                        dve.wait_ge((s_fs0, s_fs1)[b], i * 16)
                    dve.tensor_tensor(GO[:, b, hf * HD:(hf + 1) * HD], bank(6 + hf, HD), GB[b][:, hf * HD:(hf + 1) * HD], ADD).then_inc(s_f3, 1)
            expert1(0, 0, 0, False)
            expert1(1, 0, 1, False)
            with dve.Fori(1, NX // 2) as i:
                expert1(i * 2, i, 0, True)
                expert1(i * 2 + 1, i, 1, True)
            for n in range(NT):
                combine(n, 0, n, 2 * NT, 4)


_INS = ['x', 'src', 'dst', 'edge_type_3', 'node_type_3', 'L0_gnn_W1', 'L0_gnn_a_src1', 'L0_gnn_a_dst1', 'L0_gnn_b1', 'L0_gnn_W2', 'L0_gnn_a_src2', 'L0_gnn_a_dst2', 'L0_gnn_b2', 'L0_ffn_Wr', 'L0_ffn_w1', 'L0_ffn_w3', 'L0_ffn_w2', 'L0_ffn_s1', 'L0_ffn_s3', 'L0_ffn_s2', 'L1_gnn_node_emb', 'L1_gnn_w_rel1', 'L1_gnn_w_root1', 'L1_gnn_b1', 'L1_gnn_w_rel2', 'L1_gnn_w_root2', 'L1_gnn_b2', 'L1_gnn_w_rel3', 'L1_gnn_w_root3', 'L1_gnn_b3', 'L1_ffn_router_w', 'L1_ffn_w1', 'L1_ffn_b1', 'L1_ffn_w2', 'L1_ffn_b2']
_OUTS = [((1024, 768), 'float32')]


def kernel(**inputs):
    import numpy as _np
    import concourse.bacc as _bacc
    from concourse import mybir as _mybir
    from concourse.bass_utils import run_bass_kernel_spmd as _run

    nc = _bacc.Bacc("TRN2", target_bir_lowering=False, num_devices=1)
    arrays, aps = {}, {}
    for name in _INS:
        a = _np.ascontiguousarray(inputs[name])
        arrays[f"in_{name}_dram"] = a
        aps[name] = nc.dram_tensor(f"in_{name}_dram", a.shape, _mybir.dt.from_np(a.dtype), kind="ExternalInput").ap()
    shape, dtype = _OUTS[0]
    out = nc.dram_tensor("out_0_dram", shape, _mybir.dt.from_np(_np.dtype(dtype)), kind="ExternalOutput").ap()
    build(nc, aps, out)
    r = _run(nc, [arrays], core_ids=[0])
    return r.results[0]["out_0_dram"]
```
